# Optimizing a Trainium2 kernel written in Bass

```python
import numpy as np
import jax
import jax.numpy as jnp

def _softmax(x, axis=-1):
    return jax.nn.softmax(x, axis=axis)

def _gelu(x):
    return jax.nn.gelu(x, approximate=True)

def _silu(x):
    return jax.nn.silu(x)

def _sigmoid(x):
    return jax.nn.sigmoid(x)

def _layernorm(x, axis=-1, eps=1e-05):
    m = jnp.mean(x, axis=axis, keepdims=True)
    v = jnp.var(x, axis=axis, keepdims=True)
    return (x - m) / jnp.sqrt(v + eps)

def _scatter_add(tgt, idx, src, axis=0):
    return tgt.at[idx].add(src)

def _segment_sum(src, seg, n):
    return jax.ops.segment_sum(src, seg, n)
kernel_name = 'mk_gnn_resnorm_d4_gnn_r16_f038f3'

def setup_inputs(seed: int=0):
    np.random.seed(seed)
    _w = jnp.asarray

    def _rec_inputs():
        import jax
        import jax.numpy as jnp
        _gk = jax.random.key(seed)
        x = 0.4998 + 0.2888 * jax.random.normal(jax.random.fold_in(_gk, 1), (6250, 32), jnp.float32)
        src = jax.random.randint(jax.random.fold_in(_gk, 2), (200000,), 0, 6250, jnp.int32)
        dst = jnp.minimum((6250 * jax.random.uniform(jax.random.fold_in(_gk, 3), (200000,)) ** 2.0).astype(jnp.int32), 99999)
        _o = jnp.argsort(dst, stable=True)
        src = src[_o]
        dst = dst[_o]
        edge_attr_32 = -0.00010739 + 0.99994 * jax.random.normal(jax.random.fold_in(_gk, 12), (200000, 32), jnp.float32)
        edge_weight = jax.random.uniform(jax.random.fold_in(_gk, 14), (200000,), jnp.float32, 0.0, 1)
        return (x, src, dst, edge_attr_32, edge_weight)
    x, src, dst, edge_attr_32, edge_weight = _rec_inputs()

    def _L0_gnn_setup():
        import jax, jax.numpy as jnp
        import numpy as np
        NUM_LAYERS = 3
        ALPHA = 0.9
        N_NODES = 6250
        N_CLASSES = 32
        N_EDGES = 200000

        def _gcn_norm(edge_index, edge_weight, num_nodes):
            row, col = (edge_index[0], edge_index[1])
            deg = jax.ops.segment_sum(edge_weight, col, num_segments=num_nodes)
            deg_inv_sqrt = jnp.where(deg > 0, jax.lax.rsqrt(jnp.maximum(deg, 1e-38)), 0.0)
            return deg_inv_sqrt[row] * edge_weight * deg_inv_sqrt[col]
        key = jax.random.key(seed)
        k1, k2, k3 = jax.random.split(key, 3)
        y = jax.random.uniform(k1, (N_NODES, N_CLASSES), dtype=jnp.float32)
        edge_index = jax.random.randint(k2, (2, N_EDGES), 0, N_NODES, dtype=jnp.int64)
        edge_weight = jax.random.uniform(k3, (N_EDGES,), dtype=jnp.float32)
        return {'y': y, 'edge_index': edge_index, 'edge_weight': edge_weight}
    _L0_gnn_all = _L0_gnn_setup()
    _L0_gnn_in = {k: v for k, v in _L0_gnn_all.items() if k in ()}
    del _L0_gnn_all

    def _L1_gnn_setup():
        import jax, jax.numpy as jnp
        import numpy as np
        N_NODES = 6250
        N_EDGES = 25000
        D = 32
        EH = 128
        STEPS = 6

        def _gru_cell(x, h, wih, whh, bih, bhh):
            gi = x @ wih.T + bih
            gh = h @ whh.T + bhh
            ir, iz, inn = jnp.split(gi, 3, axis=-1)
            hr, hz, hn = jnp.split(gh, 3, axis=-1)
            r = jax.nn.sigmoid(ir + hr)
            z = jax.nn.sigmoid(iz + hz)
            n = jnp.tanh(inn + r * hn)
            return (1.0 - z) * n + z * h
        key = jax.random.key(seed)
        ks = jax.random.split(key, 12)
        s = 0.05
        return {'n_feat': jax.random.normal(ks[0], (N_NODES, D), jnp.float32), 'e_feat': jax.random.normal(ks[1], (N_EDGES, D), jnp.float32), 'src': jax.random.randint(ks[2], (N_EDGES,), 0, N_NODES, jnp.int32), 'dst': jax.random.randint(ks[3], (N_EDGES,), 0, N_NODES, jnp.int32), 'lin0_w': jax.random.normal(ks[4], (D, D), jnp.float32) * s, 'lin0_b': jnp.zeros((D,), jnp.float32), 'en1_w': jax.random.normal(ks[5], (EH, D), jnp.float32) * s, 'en1_b': jnp.zeros((EH,), jnp.float32), 'en2_w': jax.random.normal(ks[6], (D * D, EH), jnp.float32) * s, 'en2_b': jnp.zeros((D * D,), jnp.float32), 'conv_bias': jnp.zeros((D,), jnp.float32), 'gru_wih': jax.random.normal(ks[7], (3 * D, D), jnp.float32) * s, 'gru_whh': jax.random.normal(ks[8], (3 * D, D), jnp.float32) * s, 'gru_bih': jnp.zeros((3 * D,), jnp.float32), 'gru_bhh': jnp.zeros((3 * D,), jnp.float32)}
    _L1_gnn_all = _L1_gnn_setup()
    _L1_gnn_in = {k: v for k, v in _L1_gnn_all.items() if k in ('lin0_w', 'lin0_b', 'en1_w', 'en1_b', 'en2_w', 'en2_b', 'conv_bias', 'gru_wih', 'gru_whh', 'gru_bih', 'gru_bhh')}
    del _L1_gnn_all

    def _L2_gnn_setup():
        import jax, jax.numpy as jnp
        import numpy as np
        N_NODES = 6250
        key = jax.random.key(seed)
        k1, k2, k3, k4 = jax.random.split(key, 4)
        features = jax.random.normal(k1, (N_NODES, 32), dtype=jnp.float32)
        src = jax.random.randint(k2, (100000,), 0, N_NODES, dtype=jnp.int64)
        dst = jax.random.randint(k3, (100000,), 0, N_NODES, dtype=jnp.int64)
        weight = jax.random.normal(k4, (32, 32), dtype=jnp.float32) * (1.0 / np.sqrt(32.0))
        bias = jnp.zeros((32,), dtype=jnp.float32)
        return {'features': features, 'src': src, 'dst': dst, 'weight': weight, 'bias': bias}
    _L2_gnn_all = _L2_gnn_setup()
    _L2_gnn_in = {k: v for k, v in _L2_gnn_all.items() if k in ('weight', 'bias')}
    del _L2_gnn_all

    def _L3_gnn_setup():
        import jax, jax.numpy as jnp
        import numpy as np
        key = jax.random.key(seed)
        k1, k2 = jax.random.split(key)
        N, E, F = (6250, 100000, 32)
        edge_index = jax.random.randint(k1, (2, E), 0, N, dtype=jnp.int64)
        input_feature = jax.random.normal(k2, (N, F), dtype=jnp.float32)
        return {'edge_index': edge_index, 'input_feature': input_feature}
    _L3_gnn_all = _L3_gnn_setup()
    _L3_gnn_in = {k: v for k, v in _L3_gnn_all.items() if k in ()}
    del _L3_gnn_all
    return {'x': x, 'src': src, 'dst': dst, 'edge_attr_32': edge_attr_32, 'edge_weight': edge_weight, 'L1_gnn_lin0_w': _L1_gnn_in['lin0_w'], 'L1_gnn_lin0_b': _L1_gnn_in['lin0_b'], 'L1_gnn_en1_w': _L1_gnn_in['en1_w'], 'L1_gnn_en1_b': _L1_gnn_in['en1_b'], 'L1_gnn_en2_w': _L1_gnn_in['en2_w'], 'L1_gnn_en2_b': _L1_gnn_in['en2_b'], 'L1_gnn_conv_bias': _L1_gnn_in['conv_bias'], 'L1_gnn_gru_wih': _L1_gnn_in['gru_wih'], 'L1_gnn_gru_whh': _L1_gnn_in['gru_whh'], 'L1_gnn_gru_bih': _L1_gnn_in['gru_bih'], 'L1_gnn_gru_bhh': _L1_gnn_in['gru_bhh'], 'L2_gnn_weight': _L2_gnn_in['weight'], 'L2_gnn_bias': _L2_gnn_in['bias']}

def reference(x, src, dst, edge_attr_32, edge_weight, L1_gnn_lin0_w, L1_gnn_lin0_b, L1_gnn_en1_w, L1_gnn_en1_b, L1_gnn_en2_w, L1_gnn_en2_b, L1_gnn_conv_bias, L1_gnn_gru_wih, L1_gnn_gru_whh, L1_gnn_gru_bih, L1_gnn_gru_bhh, L2_gnn_weight, L2_gnn_bias):
    import jax
    import jax.numpy as jnp

    def _L0_gnn_ref(y, edge_index, edge_weight):
        import jax, jax.numpy as jnp
        import numpy as np
        NUM_LAYERS = 3
        ALPHA = 0.9
        N_NODES = 6250
        N_CLASSES = 32
        N_EDGES = 200000

        def _gcn_norm(edge_index, edge_weight, num_nodes):
            row, col = (edge_index[0], edge_index[1])
            deg = jax.ops.segment_sum(edge_weight, col, num_segments=num_nodes)
            deg_inv_sqrt = jnp.where(deg > 0, jax.lax.rsqrt(jnp.maximum(deg, 1e-38)), 0.0)
            return deg_inv_sqrt[row] * edge_weight * deg_inv_sqrt[col]
        num_nodes = y.shape[0]
        row, col = (edge_index[0], edge_index[1])
        norm = _gcn_norm(edge_index, edge_weight, num_nodes)
        res = (1.0 - ALPHA) * y
        out = y
        for _ in range(NUM_LAYERS):
            msg = norm[:, None] * out[row]
            agg = jax.ops.segment_sum(msg, col, num_segments=num_nodes)
            out = jnp.clip(agg * ALPHA + res, 0.0, 1.0)
        return out

    def _L1_gnn_ref(n_feat, e_feat, src, dst, lin0_w, lin0_b, en1_w, en1_b, en2_w, en2_b, conv_bias, gru_wih, gru_whh, gru_bih, gru_bhh):
        import jax, jax.numpy as jnp
        import numpy as np
        N_NODES = 6250
        N_EDGES = 25000
        D = 32
        EH = 128
        STEPS = 6

        def _gru_cell(x, h, wih, whh, bih, bhh):
            gi = x @ wih.T + bih
            gh = h @ whh.T + bhh
            ir, iz, inn = jnp.split(gi, 3, axis=-1)
            hr, hz, hn = jnp.split(gh, 3, axis=-1)
            r = jax.nn.sigmoid(ir + hr)
            z = jax.nn.sigmoid(iz + hz)
            n = jnp.tanh(inn + r * hn)
            return (1.0 - z) * n + z * h
        n_nodes = n_feat.shape[0]
        out = jax.nn.relu(n_feat @ lin0_w.T + lin0_b)
        h = out
        eh = jax.nn.relu(e_feat @ en1_w.T + en1_b)
        w_e = (eh @ en2_w.T + en2_b).reshape(-1, D, D)
        for _ in range(STEPS):
            msg = jnp.einsum('ei,eio->eo', out[src], w_e)
            agg = jax.ops.segment_sum(msg, dst, num_segments=n_nodes) + conv_bias
            m = jax.nn.relu(agg)
            h = _gru_cell(m, h, gru_wih, gru_whh, gru_bih, gru_bhh)
            out = h
        return out

    def _L2_gnn_ref(features, src, dst, weight, bias):
        import jax, jax.numpy as jnp
        import numpy as np
        N_NODES = 6250
        n = features.shape[0]
        ones = jnp.ones(src.shape[0], dtype=features.dtype)
        deg_out = jax.ops.segment_sum(ones, src, num_segments=n)
        deg_in = jax.ops.segment_sum(ones, dst, num_segments=n)
        norm_src = jax.lax.rsqrt(jnp.maximum(deg_out, 1.0))
        norm_dst = jax.lax.rsqrt(jnp.maximum(deg_in, 1.0))
        h = features * norm_src[:, None]
        msgs = h[src]
        agg = jax.ops.segment_sum(msgs, dst, num_segments=n)
        agg = agg * norm_dst[:, None]
        out = agg @ weight + bias
        return jax.nn.relu(out)

    def _L3_gnn_ref(edge_index, input_feature):
        import jax, jax.numpy as jnp
        import numpy as np
        N = input_feature.shape[0]
        row, col = (edge_index[0], edge_index[1])
        w = jnp.where(row != col, 1.0, 0.0).astype(input_feature.dtype)
        loop = jnp.arange(N, dtype=row.dtype)
        row_f = jnp.concatenate([row, loop])
        col_f = jnp.concatenate([col, loop])
        w_f = jnp.concatenate([w, jnp.ones((N,), dtype=input_feature.dtype)])
        deg = jax.ops.segment_sum(w_f, col_f, num_segments=N)
        dis = jnp.where(deg > 0, jax.lax.rsqrt(deg), 0.0)
        ew = dis[row_f] * w_f * dis[col_f]
        out = jax.ops.segment_sum(ew[:, None] * input_feature[row_f], col_f, num_segments=N)
        return out
    edge_index = jnp.stack([src, dst])
    x = _layernorm(x + _L0_gnn_ref(x, edge_index, edge_weight), axis=-1)
    x = _layernorm(x + _L1_gnn_ref(x, edge_attr_32, src, dst, L1_gnn_lin0_w, L1_gnn_lin0_b, L1_gnn_en1_w, L1_gnn_en1_b, L1_gnn_en2_w, L1_gnn_en2_b, L1_gnn_conv_bias, L1_gnn_gru_wih, L1_gnn_gru_whh, L1_gnn_gru_bih, L1_gnn_gru_bhh), axis=-1)
    x = _layernorm(x + _L2_gnn_ref(x, src, dst, L2_gnn_weight, L2_gnn_bias), axis=-1)
    x = _layernorm(x + _L3_gnn_ref(edge_index, x), axis=-1)
    return x

_drawn_inputs = setup_inputs


def setup_inputs(seed=0):
    import zlib

    import numpy as np

    out = dict(_drawn_inputs(seed))
    spreads = {'L1_gnn_lin0_b': (0.0, 0.1),
     'L1_gnn_en1_b': (0.0, 0.1),
     'L1_gnn_en2_b': (0.0, 0.1),
     'L1_gnn_conv_bias': (0.0, 0.1),
     'L1_gnn_gru_bih': (0.0, 0.1),
     'L1_gnn_gru_bhh': (0.0, 0.1),
     'L2_gnn_bias': (0.0, 0.1)}
    factors = {}
    for name, (base, spread) in spreads.items():
        noise = np.random.default_rng([zlib.crc32(name.encode()), seed]).standard_normal(out[name].shape)
        drawn = base * np.exp(spread * noise) if base else spread * noise
        out[name] = jnp.asarray(drawn.astype(out[name].dtype))
    for name, factor in factors.items():
        out[name] = (out[name] * factor).astype(out[name].dtype)
    return out
```

```python
from contextlib import ExitStack, contextmanager

import concourse.bass as bass
from concourse import mybir
from concourse.alu_op_type import AluOpType as ALU

F32 = mybir.dt.float32
BF16 = mybir.dt.bfloat16
I32 = mybir.dt.int32
U32 = mybir.dt.uint32
ACT = mybir.ActivationFunctionType
AX = mybir.AxisListType.X

P = 128
NODES, D, EDGES, K = 6250, 32, 200000, 128
EQ, ET = 125, 1600
NQ, NM = 98, 64
WN = 16
NC = NM // WN
HI, LO = 25, 16
NW = HI * LO
TC, BODIES = 8, 123
TP = 2 * TC * BODIES
OQ, OC = 123, 16
GATE = 4 * D
META = 5
ROW = META + D
STEPS0, STEPS1, ALPHA, EPS = 3, 6, 0.9, 1e-5
ST, SBODIES = 16, 50
HT, HBODIES = 40, 20
FULL = NODES // NM
REST = NODES - FULL * NM
assert EQ * ET == EDGES and TP >= EDGES // P + NW and OQ * OC == TP and NW >= NQ * NC


@contextmanager
def phase(nc, *names):
    with ExitStack() as ctx:
        sems = [ctx.enter_context(nc.semaphore(n)) for n in names]
        with nc.Block() as block:
            yield (block, *sems)
        nc.gpsimd.dma_reset()
        for s in sems:
            nc.gpsimd.sem_clear(s)
        nc.all_engine_barrier()


class Chain:

    def __init__(self, eng, sem, base=0):
        self.eng, self.sem, self.base, self.n = eng, sem, base, 0

    def __call__(self, ins):
        self.n += 1
        ins.then_inc(self.sem, 1)
        self.eng.wait_ge(self.sem, self.base + self.n)


def peeled(eng, count):
    yield 0
    with eng.Fori(1, count) as i:
        yield i


def wait_after_first(eng, sem, value):
    if not (isinstance(value, int) and value == 0):
        eng.wait_ge(sem, value)


def hold(eng, sem):
    eng.sem_inc(sem, 1)


class Mem:
    pass


def load_nodes(sp, dst, dram, sem):
    sp.dma_start(dst[0:FULL, :], dram[0:FULL * NM, :].rearrange("(q m) f -> q (m f)", m=NM)).then_inc(sem, 16)
    sp.dma_start(dst[FULL:FULL + 1, 0:REST * D],
                 dram[FULL * NM:NODES, :].rearrange("(q m) f -> q (m f)", q=1)).then_inc(sem, 16)


def prepare_edges(nc, m, src, dst, weight):
    with phase(nc, "edges_in", "prep", "iotas", "zeroed") as (block, edges_in, prep, iotas, zeroed):
        @block.sync
        def _(sp):
            sp.dma_start(m.src[:, :], src.rearrange("(q t) -> q t", t=ET)).then_inc(edges_in, 16)
            sp.dma_start(m.dst[:, :], dst.rearrange("(q t) -> q t", t=ET)).then_inc(edges_in, 16)
            sp.dma_start(m.wcol[:, :], weight.rearrange("(q t) -> q t", t=ET)).then_inc(edges_in, 16)
            sp.wait_ge(edges_in, 48)
            sp.wait_ge(zeroed, 1)
            for c in range(OC):
                sp.dma_start(m.slots.rearrange("(s t) r -> s (t r)", t=TP)[:, c * OQ * ROW:(c + 1) * OQ * ROW],
                             m.zeros[:, 0:OQ * ROW]).then_inc(edges_in, 16)
            sp.wait_ge(edges_in, 48 + 16 * OC)

        @block.gpsimd
        def _(pool):
            nc.gpsimd.iota(m.iota_i[:, :], [[1, NW]], base=0, channel_multiplier=0).then_inc(iotas, 1)
            nc.gpsimd.iota(m.pcol_i[:, :], [[1, 1]], base=0, channel_multiplier=1).then_inc(iotas, 1)

        @block.vector
        def _(dve):
            nc.vector.memset(m.zeros[:, :], 0.0).then_inc(zeroed, 1)
            do = Chain(dve, prep)
            V = nc.vector
            dve.wait_ge(iotas, 2)
            do(V.tensor_copy(m.iota[:, :], m.iota_i[:, :]))
            do(V.tensor_copy(m.pcol[:, :], m.pcol_i[:, :]))
            do(V.tensor_scalar(m.ident[:, :], m.iota[:, 0:P], m.pcol[:, 0:1], None, ALU.is_equal))
            do(V.tensor_scalar(m.earlier[:, :], m.iota[:, 0:P], m.pcol[:, 0:1], None, ALU.is_gt))
            do(V.tensor_scalar(m.others[:, :], m.iota[:, 0:P], m.pcol[:, 0:1], None, ALU.is_le))
            do(V.memset(m.ones_b[:, :], 1.0))
            do(V.memset(m.ones_f[:, :], 1.0))
            do(V.memset(m.zero_b[:, :], 0.0))
            do(V.tensor_scalar_add(m.node1[:, :], m.iota[:, 0:WN], 1.0))
            dve.wait_ge(edges_in, 48)
            meta_i = m.meta.bitcast(I32).rearrange("q (t r) -> q t r", r=META)
            meta_f = m.meta.rearrange("q (t r) -> q t r", r=META)
            do(V.tensor_copy(meta_i[:, :, 0], m.src[:, :]))
            do(V.tensor_scalar(m.tmp_i[:, :], m.dst[:, :], WN - 1, None, ALU.bitwise_and))
            do(V.tensor_scalar_add(meta_f[:, :, 1], m.tmp_i[:, :], 1.0))
            do(V.tensor_copy(meta_f[:, :, 2], m.wcol[:, :]))
            do(V.tensor_tensor(meta_f[:, :, 3], m.src[:, :], m.dst[:, :], ALU.not_equal))
            do(V.memset(meta_f[:, :, 4], 1.0))
            for out, x, shift, mask in ((m.win, m.dst, 4, 0xffff), (m.whi, m.dst, 8, 0xffff), (m.wlo, m.dst, 4, 15),
                                        (m.shi, m.src, 6, 0xffff), (m.slo, m.src, 0, 63)):
                do(V.tensor_scalar(m.tmp_i[:, :], x[:, :], shift, mask, ALU.logical_shift_right, ALU.bitwise_and))
                do(V.tensor_copy(out[:, :], m.tmp_i[:, :]))


def onehots(nc, out, digit, iota, n, w):
    return nc.vector.tensor_tensor(out, digit.unsqueeze(2).broadcast_to([EQ, n, w]),
                                   iota[0:EQ, 0:w].unsqueeze(1).broadcast_to([EQ, n, w]), ALU.is_equal)


def count_windows(nc, m):
    with phase(nc, "hots", "counted", "stored") as (block, hots, counted, stored):
        @block.vector
        def _(dve):
            with dve.Fori(0, HBODIES) as i:
                for h in range(2):
                    dve.wait_ge(counted, i * 2 + h + 1)
                    c = bass.ds(i * 2 * HT + h * HT, HT)
                    onehots(nc, m.hot_hi[h], m.whi[:, c], m.iota, HT, HI).then_inc(hots, 1)
                    onehots(nc, m.hot_lo[h], m.wlo[:, c], m.iota, HT, LO).then_inc(hots, 1)
            dve.wait_ge(counted, 2 * HBODIES + 3)
            nc.vector.tensor_copy(m.count[:, :], m.ps_count).then_inc(hots, 1)

        @block.tensor
        def _(pe):
            nc.tensor.matmul(m.ps_count, m.zero_b[0:1, 0:HI], m.zero_b[0:1, 0:LO],
                             start=True, stop=False, skip_group_check=True).then_inc(counted, 2)
            with pe.Fori(0, HBODIES) as i:
                for h in range(2):
                    pe.wait_ge(hots, i * 4 + h * 2 + 2)
                    for t in range(HT):
                        mm = nc.tensor.matmul(m.ps_count, m.hot_hi[h][:, t, :], m.hot_lo[h][:, t, :],
                                              start=False, stop=False, skip_group_check=True)
                    mm.then_inc(counted, 1)
            nc.tensor.matmul(m.ps_count, m.zero_b[0:1, 0:HI], m.zero_b[0:1, 0:LO], start=False, stop=True,
                             skip_group_check=True).then_inc(counted, 1)

        @block.sync
        def _(sp):
            sp.wait_ge(hots, 4 * HBODIES + 1)
            sp.dma_start(m.row_dram.rearrange("(h l) -> h l", l=LO), m.count[:, :]).then_inc(stored, 16)
            sp.wait_ge(stored, 16)
            sp.dma_start(m.cnt[:, :], m.row_dram.unsqueeze(0).broadcast_to([P, NW])).then_inc(stored, 16)
            sp.wait_ge(stored, 32)


def place_windows(nc, m):
    with phase(nc, "placed") as (block, placed):
        @block.vector
        def _(dve):
            do = Chain(dve, placed)
            V = nc.vector
            do(V.tensor_scalar_add(m.cnt[:, :], m.cnt[:, :], float(P - 1)))
            do(V.tensor_copy(m.cnt_i[:, :], m.cnt[:, :]))
            do(V.tensor_scalar(m.cnt_i[:, :], m.cnt_i[:, :], 7, None, ALU.logical_shift_right))
            do(V.tensor_copy(m.tiles[:, :], m.cnt_i[:, :]))
            do(V.tensor_scalar_max(m.tiles[:, :], m.tiles[:, :], 1.0))
            a, b = m.tiles, m.scan0
            shift = 1
            while shift < NW:
                do(V.tensor_copy(b[:, 0:shift], a[:, 0:shift]))
                do(V.tensor_tensor(b[:, shift:NW], a[:, shift:NW], a[:, 0:NW - shift], ALU.add))
                a, b = b, (m.scan1 if b is m.scan0 else m.scan0)
                shift *= 2
            do(V.tensor_tensor(m.first[:, :], a[:, :], m.tiles[:, :], ALU.subtract))
            do(V.tensor_scalar_mul(m.first_slot[:, :], m.first[:, :], float(P)))
            for c in range(OC):
                do(V.tensor_scalar_add(m.tnum[:, :], m.pcol[:, :], float(OQ * c)))
                do(V.tensor_scalar(b[0:OQ, :], m.first[0:OQ, :], m.tnum[0:OQ, 0:1], None, ALU.is_le))
                do(V.scalar_tensor_tensor(m.owner[:, c, :], a[0:OQ, :], m.tnum[0:OQ, 0:1], b[0:OQ, :],
                                          ALU.is_gt, ALU.mult))


def scatter_rows(nc, m, attr):
    attr_v = attr.rearrange("(q t) f -> q t f", t=ET)
    with phase(nc, "hot_ready", "ranked", "slot_read", "row_meta", "srchot", "srccount",
               "attr_a", "attr_b", "scat_a", "scat_b", "own", "held_sp", "held_pool") as (
            block, hot_ready, ranked, slot_read, row_meta, srchot, srccount, attr_a, attr_b, scat_a, scat_b, own,
            held_sp, held_pool):
        attr_in, scattered = (attr_a, attr_b), (scat_a, scat_b)

        @block.sync
        def _(sp):
            for i in peeled(sp, SBODIES):
                for h in range(2):
                    wait_after_first(sp, scattered[h], i * 16 * ST)
                    hold(sp, held_sp)
                    sp.dma_start(m.rows[h][:, :, META:ROW],
                                 attr_v[:, bass.ds(i * 2 * ST + h * ST, ST), :]).then_inc(attr_in[h], 16)

        @block.gpsimd
        def _(pool):
            with pool.Fori(0, SBODIES) as i:
                for h in range(2):
                    pool.wait_ge(row_meta, i * 2 + h + 1)
                    pool.wait_ge(attr_in[h], i * 16 + 16)
                    hold(pool, held_pool)
                    for t in range(ST):
                        nc.gpsimd.indirect_dma_start(
                            m.slots, bass.IndirectOffsetOnAxis(ap=m.slot_u[h][:, t:t + 1], axis=0),
                            m.rows[h][:, t, :], None).then_inc(scattered[h], 16)
            for h in range(2):
                pool.wait_ge(scattered[h], SBODIES * 16 * ST)

        @block.vector
        def _(dve):
            V = nc.vector
            chain = 8
            V.memset(m.ring[2], 0.0).then_inc(own, 1)
            V.memset(m.ring[3], 0.0).then_inc(hot_ready, 1)
            dve.wait_ge(own, 1)
            dve.wait_ge(hot_ready, 1)
            dve.sem_inc(slot_read, 2)
            for i in peeled(dve, SBODIES):
                for h in range(2):
                    do = Chain(dve, own, 1 + i * 2 * chain + h * chain)
                    c = bass.ds(i * 2 * ST + h * ST, ST)
                    do(V.tensor_copy(m.win_now[h], m.win[:, c]))
                    dve.wait_ge(srccount, i * 2 + h + 1)
                    onehots(nc, m.hot_shi[h], m.shi[:, c], m.iota, ST, NQ).then_inc(srchot, 1)
                    onehots(nc, m.hot_slo[h], m.slo[:, c], m.iota, ST, NM).then_inc(srchot, 1)

                    def hot(t):
                        V.tensor_scalar(m.ring[(h * ST + t) % 4], m.iota_h[0:EQ, :], m.win_now[h][:, t:t + 1], None,
                                        ALU.is_equal).then_inc(hot_ready, 1)

                    hot(0)
                    for t in range(ST):
                        if t + 1 < ST:
                            hot(t + 1)
                        n = i * 2 * ST + h * ST + t
                        dve.wait_ge(ranked, n + 1)
                        ins = V.tensor_tensor_reduce(
                            out=m.junk[t % 2], in0=m.ring[(h * ST + t) % 4], in1=m.ps_rank[t % 2],
                            scale=1.0, scalar=0.0, op0=ALU.mult, op1=ALU.add, accum_out=m.slot_f[h][:, t:t + 1])
                        ins.then_inc(slot_read, 1)
                    dve.wait_ge(slot_read, i * 2 * ST + h * ST + ST + 2)
                    do(V.tensor_copy(m.slot_i, m.slot_f[h]))
                    do(V.tensor_scalar(m.slot_t, m.slot_i, 7, None, ALU.logical_shift_right))
                    do(V.tensor_scalar(m.slot_p, m.slot_i, P - 1, None, ALU.bitwise_and))
                    do(V.tensor_copy(m.slot_tf, m.slot_t))
                    do(V.tensor_copy(m.slot_pf, m.slot_p))
                    wait_after_first(dve, scattered[h], i * 16 * ST)
                    do(V.scalar_tensor_tensor(m.slot_u[h], m.slot_pf, float(TP), m.slot_tf, ALU.mult, ALU.add))
                    do(V.tensor_copy(m.rows[h][:, :, 0:META],
                                     m.meta[:, bass.ds((i * 2 * ST + h * ST) * META, ST * META)]
                                     .rearrange("q (t r) -> q t r", r=META)))
                    dve.sem_inc(row_meta, 1)
                    assert do.n == chain
            dve.wait_ge(srccount, 2 * SBODIES + 3)
            V.tensor_copy(m.deg_out[:, :], m.ps_src).then_inc(own, 1)

        @block.tensor
        def _(pe):
            mm = nc.tensor.matmul
            for b in range(2):
                mm(m.ps_rank[b], m.ones_f[0:1, 0:EQ], m.first_slot[0:1, :], start=True, stop=False,
                   skip_group_check=True)
            mm(m.ps_src, m.zero_b[0:1, 0:NQ], m.zero_b[0:1, 0:NM], start=True, stop=False,
               skip_group_check=True).then_inc(srccount, 2)
            with pe.Fori(0, SBODIES) as i:
                for h in range(2):
                    pe.wait_ge(srchot, i * 4 + h * 2 + 2)
                    for t in range(ST):
                        s = mm(m.ps_src, m.hot_shi[h][:, t, :], m.hot_slo[h][:, t, :], start=False, stop=False,
                               skip_group_check=True)
                    s.then_inc(srccount, 1)
                    for t in range(ST):
                        n = i * 2 * ST + h * ST + t
                        now, r = m.ps_rank[t % 2], h * ST + t
                        pe.wait_ge(hot_ready, n + 2)
                        pe.wait_ge(slot_read, n + 1)
                        mm(now, m.others[0:EQ, 0:EQ], m.ring[(r + 2) % 4], start=False, stop=False,
                           skip_group_check=True)
                        mm(now, m.ones_b[0:EQ, 0:EQ], m.ring[(r + 3) % 4], start=False, stop=False,
                           skip_group_check=True)
                        mm(now, m.earlier[0:EQ, 0:EQ], m.ring[r % 4], start=False, stop=True,
                           skip_group_check=True).then_inc(ranked, 1)
            mm(m.ps_src, m.zero_b[0:1, 0:NQ], m.zero_b[0:1, 0:NM], start=False, stop=True,
               skip_group_check=True).then_inc(srccount, 1)


def encode_edges(nc, m):
    slots_v = m.slots.rearrange("(s t) r -> s (t r)", t=TP)
    with phase(nc, "rows_a", "rows_b", "meta_kept", "masked", "degs", "turned", "turned_sb", "eh_ps",
               "biased", "relu", "eh_out_a", "eh_out_b", "deg_sb", "deg_out_a", "deg_out_b", "held_sp") as (
            block, rows_a, rows_b, meta_kept, masked, degs, turned, turned_sb, eh_ps, biased, relu,
            eh_out_a, eh_out_b, deg_sb, deg_out_a, deg_out_b, held_sp):
        rows_in, eh_out, deg_out = (rows_a, rows_b), (eh_out_a, eh_out_b), (deg_out_a, deg_out_b)

        @block.sync
        def _(sp):
            with sp.Fori(0, BODIES) as i:
                for h in range(2):
                    n = i * 2 + h
                    sp.wait_ge(meta_kept, n * 2 + 2)
                    hold(sp, held_sp)
                    sp.wait_ge(degs, n + 1)
                    hold(sp, held_sp)
                    sp.dma_start(m.rowin[h], slots_v[:, bass.ds(n * TC * ROW, TC * ROW)]).then_inc(rows_in[h], 16)

        @block.vector
        def _(dve):
            V = nc.vector
            dve.sem_inc(meta_kept, 4)
            dve.sem_inc(biased, 2)
            with dve.Fori(0, BODIES) as i:
                for h in range(2):
                    n = i * 2 + h
                    dve.wait_ge(rows_in[h], i * 16 + 16)
                    rows = m.rowin[h].rearrange("s (t r) -> s t r", r=ROW)
                    V.tensor_copy(m.meta_t[:, bass.ds(n * TC * 4, TC * 4)].rearrange("s (t r) -> s t r", r=4),
                                  rows[:, :, 0:4]).then_inc(meta_kept, 1)
                    dve.wait_ge(turned, n * 2 + 2)
                    V.tensor_copy(m.attr[h].rearrange("s (t f) -> s t f", f=D),
                                  rows[:, :, META:ROW]).then_inc(meta_kept, 1)
                    dve.wait_ge(degs, n + 1)
                    V.tensor_tensor(m.mask[h], rows[:, :, 1].unsqueeze(2).broadcast_to([P, TC, WN]),
                                    m.node1[:, :].unsqueeze(1).broadcast_to([P, TC, WN]),
                                    ALU.is_equal).then_inc(masked, 1)
                    for g in range(2):
                        dve.wait_ge(eh_ps, n * 2 + g + 3)
                        dve.wait_ge(relu, n * 2 + g + 1)
                        V.tensor_tensor(m.eh_pre[g], m.ps_eh[g], m.en1_b[:, :], ALU.add).then_inc(biased, 1)

        @block.tensor
        def _(pe):
            pe.sem_inc(degs, 2)
            pe.sem_inc(turned, 4)
            pe.sem_inc(eh_ps, 2)
            with pe.Fori(0, BODIES) as i:
                for h in range(2):
                    n = i * 2 + h
                    rows = m.rowin[h].rearrange("s (t r) -> s t r", r=ROW)
                    pe.wait_ge(rows_in[h], i * 16 + 16)
                    pe.wait_ge(meta_kept, n * 2 + 6)
                    for g in range(2):
                        pe.wait_ge(turned_sb, n * 2 + g + 1)
                        nc.tensor.transpose(m.ps_turn[g], m.attr[h][:, g * P:(g + 1) * P],
                                            m.ident[:, :]).then_inc(turned, 1)
                    pe.wait_ge(masked, n + 1)
                    pe.wait_ge(deg_sb, n + 1)
                    for t in range(TC):
                        s = nc.tensor.matmul(m.ps_deg[:, t * WN:(t + 1) * WN], rows[:, t, 2:META],
                                             m.mask[h][:, t, :], start=True, stop=True)
                    s.then_inc(degs, 1)
                    for g in range(2):
                        pe.wait_ge(turned_sb, n * 2 + g + 3)
                        pe.wait_ge(biased, n * 2 + g + 1)
                        nc.tensor.matmul(m.ps_eh[g], m.attr_t[g], m.en1[:, :], start=True,
                                         stop=True).then_inc(eh_ps, 1)

        @block.scalar
        def _(act):
            act.sem_inc(turned_sb, 2)
            act.sem_inc(relu, 2)
            act.sem_inc(deg_sb, 1)
            for i in peeled(act, BODIES):
                for h in range(2):
                    n = i * 2 + h
                    for g in range(2):
                        act.wait_ge(turned, n * 2 + g + 5)
                        act.wait_ge(eh_ps, n * 2 + g + 1)
                        nc.scalar.activation(m.attr_t[g], m.ps_turn[g], ACT.Copy).then_inc(turned_sb, 1)
                    act.wait_ge(degs, n + 3)
                    wait_after_first(act, deg_out[h], i * 16)
                    nc.scalar.activation(m.deg_s[h], m.ps_deg, ACT.Copy).then_inc(deg_sb, 1)
                    act.wait_ge(deg_sb, n + 2)
                    act.dma_start(m.deg_dram[:, bass.ds(n * TC * WN, TC * WN)], m.deg_s[h]).then_inc(deg_out[h], 16)
                    wait_after_first(act, eh_out[h], i * 16)
                    for g in range(2):
                        act.wait_ge(biased, n * 2 + g + 3)
                        nc.scalar.activation(m.eh[h][:, g * 4 * K:(g + 1) * 4 * K], m.eh_pre[g],
                                             ACT.Relu).then_inc(relu, 1)
                    act.wait_ge(relu, n * 2 + 4)
                    act.dma_start(m.eh_dram[:, bass.ds(n * TC * K, TC * K)], m.eh[h]).then_inc(eh_out[h], 16)
            for h in range(2):
                act.wait_ge(eh_out[h], BODIES * 16)
                act.wait_ge(deg_out[h], BODIES * 16)


def owner_of(m, ch, c):
    return m.owner[:, ch, 0:NQ * NC].rearrange("t (q c) -> t c q", c=NC)[:, c, :]


def node_degrees(nc, m):
    with phase(nc, "deg_in", "summed", "copied", "rooted", "own") as (block, deg_in, summed, copied, rooted, own):
        @block.sync
        def _(sp):
            for j in range(3):
                sp.dma_start(m.deg_t[:, :, j * WN:(j + 1) * WN],
                             m.deg_dram[j, :].rearrange("(ch t n) -> t ch n", t=OQ, n=WN)).then_inc(deg_in, 16)

        @block.tensor
        def _(pe):
            pe.wait_ge(deg_in, 48)
            for c in range(NC):
                for ch in range(OC):
                    mm = nc.tensor.matmul(m.ps_degree[:, c * 3 * WN:(c + 1) * 3 * WN], owner_of(m, ch, c),
                                          m.deg_t[:, ch, :], start=(ch == 0), stop=(ch == OC - 1))
            mm.then_inc(summed, 1)

        @block.vector
        def _(dve):
            V = nc.vector
            do = Chain(dve, own)
            dve.wait_ge(summed, 1)
            psd = m.ps_degree.rearrange("q (c j n) -> q c j n", c=NC, j=3)
            per = lambda x: x.rearrange("q (c n) -> q c n", c=NC)
            do(V.tensor_copy(per(m.deg_w), psd[:, :, 0, :]))
            do(V.tensor_scalar(m.positive, m.deg_w, 0.0, 2.0 ** 15, ALU.is_gt, ALU.mult))
            do(V.tensor_scalar_max(m.deg_w, m.deg_w, 1e-38))
            do(V.tensor_scalar_add(per(m.inv_self), psd[:, :, 1, :], 1.0))
            do(V.tensor_scalar_max(per(m.inv_in), psd[:, :, 2, :], 1.0))
            do(V.tensor_scalar_max(m.inv_out, m.deg_out[:, :], 1.0))
            dve.sem_inc(copied, 1)
            dve.wait_ge(rooted, 4)
            for x in (m.deg_w, m.inv_self, m.inv_in, m.inv_out):
                do(V.reciprocal(x, x))
            do(V.tensor_tensor(m.inv_w, m.deg_w, m.positive, ALU.mult))

        @block.scalar
        def _(act):
            act.wait_ge(copied, 1)
            nc.scalar.activation(m.deg_w, m.deg_w, ACT.Sqrt, scale=2.0 ** 30).then_inc(rooted, 1)
            for x in (m.inv_self, m.inv_in, m.inv_out):
                nc.scalar.activation(x, x, ACT.Sqrt).then_inc(rooted, 1)


def edge_pass(nc, m, weight, after, edge_matrices=False):
    per = 2 if weight is not None else 1
    with phase(nc, "idx_ready", "gath_a", "gath_b", "masked", "made", "summed", "g_done", "g_sb", "eh_a", "eh_b",
               "s_sb", "projected", "p_sb", "st_a", "st_b", "held_sp", "held_pool") as (
            block, idx_ready, gath_a, gath_b, masked, made, summed, g_done, g_sb, eh_a, eh_b,
            s_sb, projected, p_sb, st_a, st_b, held_sp, held_pool):
        gathered, eh_in, stored = (gath_a, gath_b), (eh_a, eh_b), (st_a, st_b)
        GT = 16 * TC

        @block.gpsimd
        def _(pool):
            with pool.Fori(0, BODIES) as i:
                for h in range(2):
                    n = i * 2 + h
                    pool.wait_ge(idx_ready, n + 1)
                    pool.wait_ge(summed, n + 1)
                    if edge_matrices:
                        pool.wait_ge(made, n + 1)
                    hold(pool, held_pool)
                    for t in range(TC):
                        nc.gpsimd.indirect_dma_start(
                            m.xs[h][:, t * D:(t + 1) * D], None, m.node_dram,
                            bass.IndirectOffsetOnAxis(ap=m.idx[h][:, t:t + 1], axis=0)).then_inc(gathered[h], 16)
            for h in range(2):
                pool.wait_ge(gathered[h], BODIES * GT)

        @block.sync
        def _(sp):
            if edge_matrices:
                with sp.Fori(0, BODIES) as i:
                    for h in range(2):
                        n = i * 2 + h
                        sp.wait_ge(g_done, n * TC + TC)
                        hold(sp, held_sp)
                        sp.dma_start(m.eh[h], m.eh_dram[:, bass.ds(n * TC * K, TC * K)]).then_inc(eh_in[h], 16)

        @block.vector
        def _(dve):
            V = nc.vector
            if edge_matrices:
                dve.sem_inc(made, 2)

            def meta(n, word):
                return m.meta_t[:, bass.ds(n * TC * 4, TC * 4)].rearrange("s (t r) -> s t r", r=4)[:, :, word]

            for i in peeled(dve, BODIES):
                for h in range(2):
                    n = i * 2 + h
                    wait_after_first(dve, gathered[h], i * GT)
                    V.tensor_copy(m.idx[h].bitcast(F32), meta(n, 0)).then_inc(idx_ready, 1)
                    dve.wait_ge(summed, n + 1)
                    if edge_matrices:
                        dve.wait_ge(made, n + 1)
                    V.tensor_tensor(m.mask[h], meta(n, 1).unsqueeze(2).broadcast_to([P, TC, WN]),
                                    m.node1[:, :].unsqueeze(1).broadcast_to([P, TC, WN]),
                                    ALU.is_equal).then_inc(masked, 1)
                    if weight is not None:
                        dve.wait_ge(masked, n * 2 + 1)
                        V.tensor_tensor(m.mask[h], m.mask[h], meta(n, weight).unsqueeze(2).broadcast_to([P, TC, WN]),
                                        ALU.mult).then_inc(masked, 1)
                    if edge_matrices and h == 1:
                        for hh in range(2):
                            nn = i * 2 + hh
                            dve.wait_ge(masked, nn + 1)
                            dve.wait_ge(gathered[hh], i * GT + GT)
                            dve.wait_ge(g_done, nn * TC + TC)
                            V.tensor_tensor(
                                m.spread[hh],
                                m.xs[hh].rearrange("s (t i) -> s t i", i=D).unsqueeze(3).broadcast_to([P, TC, D, WN]),
                                m.mask[hh].unsqueeze(2).broadcast_to([P, TC, D, WN]), ALU.mult).then_inc(made, 1)

        @block.tensor
        def _(pe):
            mm = nc.tensor.matmul
            pe.sem_inc(summed, 2)
            pe.sem_inc(projected, 2)
            if edge_matrices:
                pe.sem_inc(g_done, 2 * TC)
            with pe.Fori(0, BODIES) as i:
                for h in range(2):
                    n = i * 2 + h
                    pe.wait_ge(gathered[h], i * GT + GT)
                    pe.wait_ge(masked, n * per + per)
                    pe.wait_ge(s_sb, n + 1)
                    for t in range(TC):
                        s = mm(m.ps_s[h][:, t * WN:(t + 1) * WN], m.xs[h][:, t * D:(t + 1) * D],
                               m.mask[h][:, t, :], start=True, stop=True)
                    s.then_inc(summed, 1)
                    if edge_matrices:
                        pe.wait_ge(eh_in[h], i * 16 + 16)
                        pe.wait_ge(made, n + 3)
                        for t in range(TC):
                            pe.wait_ge(g_sb, n * TC + t + 1)
                            mm(m.ps_g[:, t % 4, :], m.eh[h][:, t * K:(t + 1) * K], m.spread[h][:, t, :, :],
                               start=True, stop=True).then_inc(g_done, 1)
                for h in range(2):
                    n = i * 2 + h
                    pe.wait_ge(s_sb, n + 3)
                    pe.wait_ge(p_sb, n + 1)
                    if edge_matrices:
                        pe.wait_ge(g_sb, n * TC + TC + 4)
                        for d in range(D):
                            mm(m.ps_p[h], m.g[h][:, d, :, :].rearrange("k t n -> k (t n)"), m.en2[:, d, :], start=(d == 0), stop=False)
                    mm(m.ps_p[h], m.s[h], after, start=not edge_matrices, stop=True).then_inc(projected, 1)

        @block.scalar
        def _(act):
            copy = ACT.Copy
            act.sem_inc(s_sb, 2)
            act.sem_inc(p_sb, 2)
            if edge_matrices:
                act.sem_inc(g_sb, 4)
            for i in peeled(act, BODIES):
                for h in range(2):
                    n = i * 2 + h
                    act.wait_ge(summed, n + 3)
                    act.wait_ge(projected, n + 1)
                    nc.scalar.activation(m.s[h], m.ps_s[h], copy).then_inc(s_sb, 1)
                    if edge_matrices:
                        for t in range(TC):
                            act.wait_ge(g_done, n * TC + t + 1 + 2 * TC)
                            nc.scalar.activation(
                                m.g[h][:, :, t, :], m.ps_g[:, t % 4, :].rearrange("k (i n) -> k i n", n=WN), copy).then_inc(g_sb, 1)
                for h in range(2):
                    n = i * 2 + h
                    act.wait_ge(projected, n + 3)
                    wait_after_first(act, stored[h], i * 16)
                    nc.scalar.activation(m.part[h], m.ps_p[h], copy).then_inc(p_sb, 1)
                    act.wait_ge(p_sb, n + 3)
                    act.dma_start(m.part_dram[bass.ds(n * TC * WN, TC * WN), :], m.part[h]).then_inc(stored[h], 16)
            for h in range(2):
                act.wait_ge(stored[h], BODIES * 16)


def add_tiles(nc, m):
    with phase(nc, "parts_in", "agg") as (block, parts_in, agg):
        @block.sync
        def _(sp):
            parts = m.part_dram.rearrange("(ch t n) o -> t ch (n o)", t=OQ, n=WN)
            sp.dma_start(m.parts, parts).then_inc(parts_in, 16)
            sp.wait_ge(parts_in, 16)

        @block.tensor
        def _(pe):
            pe.wait_ge(parts_in, 16)
            for c in range(NC):
                for ch in range(OC):
                    mm = nc.tensor.matmul(m.agg[c], owner_of(m, ch, c), m.parts[:, ch, :],
                                          start=(ch == 0), stop=(ch == OC - 1))
            mm.then_inc(agg, 1)
            pe.wait_ge(agg, 1)


def by_node(x, rows=NM):
    return x.unsqueeze(2).broadcast_to([NQ, rows, D])


def by_feature(x, rows=NM):
    return x[:, 0:D].unsqueeze(1).broadcast_to([NQ, rows, D])


def feats(x):
    return x.rearrange("q (m f) -> q m f", f=D)


def layer_norm(nc, m, do, to_act, from_act, x, y):
    V = nc.vector
    do(V.tensor_tensor(x, x, y, ALU.add))
    do(V.tensor_reduce(m.stat, feats(x), AX, ALU.add))
    do(V.tensor_scalar_mul(m.stat, m.stat, 1.0 / D))
    do(V.tensor_tensor(feats(x), feats(x), by_node(m.stat), ALU.subtract))
    do(V.tensor_tensor(y, x, x, ALU.mult))
    do(V.tensor_reduce(m.stat, feats(y), AX, ALU.add))
    do(V.tensor_scalar(m.stat, m.stat, 1.0 / D, EPS, ALU.mult, ALU.add))
    do.eng.sem_inc(to_act, 1)
    do.eng.wait_ge(from_act, 1)
    do(V.reciprocal(m.stat, m.stat))
    do(V.tensor_tensor(feats(x), feats(x), by_node(m.stat), ALU.mult))


def root_for_norm(nc, m, act, to_act, from_act):
    act.wait_ge(to_act, 1)
    nc.scalar.activation(m.stat, m.stat, ACT.Sqrt).then_inc(from_act, 1)


def store_nodes(sp, m, x, ready, sem):
    sp.wait_ge(ready, 1)
    sp.dma_start(m.node_dram.rearrange("(q m) f -> q (m f)", m=NM), x).then_inc(sem, 16)
    sp.wait_ge(sem, 16)


def load_everything(nc, m, x, w):
    with phase(nc, "cleared", "loaded") as (block, cleared, loaded):
        @block.vector
        def _(dve):
            do = Chain(dve, cleared)
            for t in (m.x, m.en1, m.lin0, m.gru_i, m.gru_h):
                do(nc.vector.memset(t, 0.0))

        @block.sync
        def _(sp):
            sp.wait_ge(cleared, 5)
            n = 0

            def load(out, in_):
                nonlocal n
                sp.dma_start(out, in_).then_inc(loaded, 16)
                n += 16

            def spread(x, rows, times):
                return x.unsqueeze(0).unsqueeze(0).broadcast_to([rows, times, x.shape[0]])

            load_nodes(sp, m.x, x, loaded)
            n += 32
            load(m.en2.rearrange("k i o -> k (i o)"), w["en2"])
            load(m.en2_b, w["en2_b"].rearrange("(i o) -> i o", o=D))
            load(m.w2, w["w2"])
            load(m.b2, w["b2"].unsqueeze(0).broadcast_to([NQ, D]))
            load(m.conv_b, w["conv_b"].unsqueeze(0).broadcast_to([NQ, D]))
            load(m.lin0_b, w["lin0_b"].unsqueeze(0).broadcast_to([NQ, D]))
            load(m.en1_b.rearrange("p (j k) -> p j k", k=K), spread(w["en1_b"], P, 4))
            for dst, src, a, b in ((m.bias_i, "bih", 0, 2 * D), (m.bias_h, "bhh", 0, 2 * D)):
                load(dst, w[src].unsqueeze(0).broadcast_to([NQ, 3 * D]))
            for j in range(4):
                rows = slice(D * j, D * (j + 1))
                load(m.en1[rows, j * K:(j + 1) * K], w["en1"])
                load(m.lin0[rows, j * D:(j + 1) * D], w["lin0"])
                load(m.gru_i[rows, j * GATE:j * GATE + 3 * D], w["wih"])
                load(m.gru_h[rows, j * GATE:j * GATE + 2 * D], w["whh"][:, 0:2 * D])
                load(m.gru_h[rows, j * GATE + 3 * D:(j + 1) * GATE], w["whh"][:, 2 * D:3 * D])
            sp.wait_ge(loaded, n)
    with phase(nc, "own") as (block, own):
        @block.vector
        def _(dve):
            do = Chain(dve, own)
            V = nc.vector
            do(V.tensor_tensor(m.gate_b[:, 0:2 * D], m.bias_i[:, 0:2 * D], m.bias_h[:, 0:2 * D], ALU.add))
            do(V.tensor_copy(m.gate_b[:, 2 * D:3 * D], m.bias_i[:, 2 * D:3 * D]))
            do(V.tensor_copy(m.gate_b[:, 3 * D:GATE], m.bias_h[:, 2 * D:3 * D]))


def propagate(nc, m):
    def scaled_state(src):
        with phase(nc, "ready", "stored", "own") as (block, ready, stored, own):
            @block.vector
            def _(dve):
                do = Chain(dve, own)
                do(nc.vector.tensor_tensor(feats(m.y), feats(src), by_node(m.inv_w), ALU.mult))
                dve.sem_inc(ready, 1)

            @block.sync
            def _(sp):
                store_nodes(sp, m, m.y, ready, stored)

    scaled_state(m.x)
    with nc.Fori(0, STEPS0):
        edge_pass(nc, m, 2, m.ident[0:D, 0:D])
        add_tiles(nc, m)
        with phase(nc, "ready", "stored", "own") as (block, ready, stored, own):
            @block.vector
            def _(dve):
                V = nc.vector
                do = Chain(dve, own)
                do(V.tensor_scalar_mul(m.y, m.x, 1.0 - ALPHA))
                for c in range(NC):
                    part = slice(c * WN * D, (c + 1) * WN * D)
                    do(V.tensor_tensor(feats(m.h[:, part]), feats(m.agg[c]),
                                       by_node(m.inv_w[:, c * WN:(c + 1) * WN], WN), ALU.mult))
                do(V.scalar_tensor_tensor(m.h, m.h, ALPHA, m.y, ALU.mult, ALU.add))
                do(V.tensor_scalar(m.h, m.h, 0.0, 1.0, ALU.max, ALU.min))
                do(V.tensor_tensor(feats(m.y), feats(m.h), by_node(m.inv_w), ALU.mult))
                dve.sem_inc(ready, 1)

            @block.sync
            def _(sp):
                store_nodes(sp, m, m.y, ready, stored)
    norm_phase(nc, m)


def norm_phase(nc, m):
    with phase(nc, "to_act", "from_act", "own") as (block, to_act, from_act, own):
        @block.vector
        def _(dve):
            layer_norm(nc, m, Chain(dve, own), to_act, from_act, m.x, m.h)

        @block.scalar
        def _(act):
            root_for_norm(nc, m, act, to_act, from_act)


def turn(nc, m, pe, x, out_i, turned, turned_sb):
    for c in range(NC):
        s = out_i * NC + c
        if s >= 2:
            pe.wait_ge(turned_sb, s - 1)
        for j in range(4):
            mm = nc.tensor.transpose(m.ps_s2[s % 2][:, j * NQ:(j + 1) * NQ], x[:, (4 * c + j) * P:(4 * c + j + 1) * P],
                                     m.ident[0:NQ, 0:NQ])
        mm.then_inc(turned, 1)


def copy_turned(nc, m, act, out, out_i, turned, turned_sb):
    for c in range(NC):
        s = out_i * NC + c
        act.wait_ge(turned, s + 1)
        nc.scalar.activation(out[:, 4 * c:4 * c + 4, :], m.ps_s2[s % 2][:, 0:4 * NQ].rearrange("p (j q) -> p j q", q=NQ),
                             ACT.Copy).then_inc(turned_sb, 1)


def first_state(nc, m):
    with phase(nc, "turned", "turned_sb", "out_ps", "biased", "ready", "stored") as (
            block, turned, turned_sb, out_ps, biased, ready, stored):
        @block.tensor
        def _(pe):
            turn(nc, m, pe, m.x, 0, turned, turned_sb)
            pe.wait_ge(turned_sb, NC)
            for c in range(NC):
                for j in range(4):
                    mm = nc.tensor.matmul(m.agg[c][:, j * P:(j + 1) * P], m.turned_m[:, 4 * c + j, :], m.lin0,
                                          start=True, stop=True)
            mm.then_inc(out_ps, 1)

        @block.scalar
        def _(act):
            copy_turned(nc, m, act, m.turned_m, 0, turned, turned_sb)
            act.wait_ge(biased, NC)
            nc.scalar.activation(m.h, m.h, ACT.Relu).then_inc(ready, 1)

        @block.vector
        def _(dve):
            dve.wait_ge(out_ps, 1)
            for c in range(NC):
                nc.vector.tensor_tensor(feats(m.h[:, c * WN * D:(c + 1) * WN * D]), feats(m.agg[c]),
                                        by_feature(m.lin0_b, WN), ALU.add).then_inc(biased, 1)

        @block.sync
        def _(sp):
            store_nodes(sp, m, m.h, ready, stored)


def gru(nc, m):
    gates = m.gates.rearrange("q (m g) -> q m g", g=GATE)
    part = lambda j: gates[:, :, j * D:(j + 1) * D]
    with phase(nc, "biased", "relu", "turned", "turned_sb", "gate_ps", "gate_sb", "sig", "pre_n", "tanh",
               "ready", "stored", "own") as (
            block, biased, relu, turned, turned_sb, gate_ps, gate_sb, sig, pre_n, tanh, ready, stored, own):
        @block.vector
        def _(dve):
            V = nc.vector
            do = Chain(dve, own)
            for c in range(NC):
                V.tensor_tensor(feats(m.y[:, c * WN * D:(c + 1) * WN * D]), feats(m.agg[c]),
                                by_feature(m.conv_b, WN), ALU.add).then_inc(biased, 1)
            for g in range(16):
                dve.wait_ge(gate_ps, g + 1)
                V.tensor_tensor(gates[:, 4 * g:4 * g + 4, :], m.ps_p2[g % 2].rearrange("q (m g) -> q m g", g=GATE),
                                m.gate_b.unsqueeze(1).broadcast_to([NQ, 4, GATE]), ALU.add).then_inc(gate_sb, 1)
            dve.wait_ge(sig, 1)
            do(V.tensor_tensor(part(0), part(0), part(3), ALU.mult))
            do(V.tensor_tensor(part(2), part(2), part(0), ALU.add))
            dve.sem_inc(pre_n, 1)
            dve.wait_ge(tanh, 1)
            do(V.tensor_tensor(feats(m.y), feats(m.h), part(2), ALU.subtract))
            do(V.tensor_tensor(feats(m.y), feats(m.y), part(1), ALU.mult))
            do(V.tensor_tensor(feats(m.h), feats(m.y), part(2), ALU.add))
            dve.sem_inc(ready, 1)

        @block.scalar
        def _(act):
            copy_turned(nc, m, act, m.turned_h, 0, turned, turned_sb)
            for c in range(NC):
                act.wait_ge(biased, c + 1)
                piece = m.y[:, c * WN * D:(c + 1) * WN * D]
                nc.scalar.activation(piece, piece, ACT.Relu).then_inc(relu, 1)
            copy_turned(nc, m, act, m.turned_m, 1, turned, turned_sb)
            act.wait_ge(gate_sb, 16)
            nc.scalar.activation(gates[:, :, 0:2 * D], gates[:, :, 0:2 * D], ACT.Sigmoid).then_inc(sig, 1)
            act.wait_ge(pre_n, 1)
            nc.scalar.activation(part(2), part(2), ACT.Tanh).then_inc(tanh, 1)

        @block.tensor
        def _(pe):
            turn(nc, m, pe, m.h, 0, turned, turned_sb)
            pe.wait_ge(relu, NC)
            turn(nc, m, pe, m.y, 1, turned, turned_sb)
            pe.wait_ge(turned_sb, 2 * NC)
            for g in range(16):
                if g >= 2:
                    pe.wait_ge(gate_sb, g - 1)
                nc.tensor.matmul(m.ps_p2[g % 2], m.turned_m[:, g, :], m.gru_i, start=True, stop=False)
                nc.tensor.matmul(m.ps_p2[g % 2], m.turned_h[:, g, :], m.gru_h, start=False,
                                 stop=True).then_inc(gate_ps, 1)

        @block.sync
        def _(sp):
            store_nodes(sp, m, m.h, ready, stored)


def convolve(nc, m):
    first_state(nc, m)
    with nc.Fori(0, STEPS1):
        edge_pass(nc, m, None, m.en2_b, edge_matrices=True)
        add_tiles(nc, m)
        gru(nc, m)
    norm_phase(nc, m)


def scale_and_store(nc, m, by):
    with phase(nc, "ready", "stored", "own") as (block, ready, stored, own):
        @block.vector
        def _(dve):
            Chain(dve, own)(nc.vector.tensor_tensor(feats(m.y), feats(m.x), by_node(by), ALU.mult))
            dve.sem_inc(ready, 1)

        @block.sync
        def _(sp):
            store_nodes(sp, m, m.y, ready, stored)


def graph_conv(nc, m):
    scale_and_store(nc, m, m.inv_out)
    edge_pass(nc, m, None, m.w2)
    add_tiles(nc, m)
    with phase(nc, "own") as (block, own):
        @block.vector
        def _(dve):
            V = nc.vector
            do = Chain(dve, own)
            for c in range(NC):
                do(V.tensor_tensor(feats(m.h[:, c * WN * D:(c + 1) * WN * D]), feats(m.agg[c]),
                                   by_node(m.inv_in[:, c * WN:(c + 1) * WN], WN), ALU.mult))
            do(V.tensor_tensor(feats(m.h), feats(m.h), by_feature(m.b2), ALU.add))
            do(V.tensor_scalar_max(m.h, m.h, 0.0))
    norm_phase(nc, m)


def self_loop_conv(nc, m):
    scale_and_store(nc, m, m.inv_self)
    edge_pass(nc, m, 3, m.ident[0:D, 0:D])
    add_tiles(nc, m)
    with phase(nc, "own") as (block, own):
        @block.vector
        def _(dve):
            V = nc.vector
            do = Chain(dve, own)
            for c in range(NC):
                part = slice(c * WN * D, (c + 1) * WN * D)
                do(V.tensor_tensor(m.h[:, part], m.agg[c], m.y[:, part], ALU.add))
            do(V.tensor_tensor(feats(m.h), feats(m.h), by_node(m.inv_self), ALU.mult))
    norm_phase(nc, m)


def store_result(nc, m, out):
    with phase(nc, "stored") as (block, stored):
        @block.sync
        def _(sp):
            sp.dma_start(out[0:FULL * NM, :].rearrange("(q m) f -> q (m f)", m=NM),
                         m.x[0:FULL, :]).then_inc(stored, 16)
            sp.dma_start(out[FULL * NM:NODES, :].rearrange("(q m) f -> q (m f)", q=1),
                         m.x[FULL:FULL + 1, 0:REST * D]).then_inc(stored, 16)
            sp.wait_ge(stored, 32)


def build(nc, x, src, dst, attr, weight, w, out):
    m = Mem()
    with ExitStack() as whole:
        def make(stack):
            def sb(name, shape, dt=F32, halves=0):
                if halves:
                    return [stack.enter_context(nc.sbuf_tensor(f"sb_{name}{i}", shape, dt))[:] for i in range(halves)]
                return stack.enter_context(nc.sbuf_tensor(f"sb_{name}", shape, dt))[:]
            return sb

        sb = make(whole)
        dram = lambda name, shape, dt=F32: nc.dram_tensor(name, shape, dt, kind="Internal").ap()
        m.slots = dram("slots", [P * TP, ROW])
        m.eh_dram = dram("eh", [P, TP * K])
        m.node_dram = dram("node_rows", [NQ * NM, D])
        m.part_dram = dram("parts", [TP * WN, D])
        m.deg_dram = dram("degree_parts", [3, TP * WN])
        m.row_dram = dram("window_counts", [NW])

        psum = lambda name, n: whole.enter_context(nc.psum_tensor(name, [P, n, 512], F32))[:]
        banks4, banks_s, banks_p = psum("banks4", 4), psum("banks_s", 2), psum("banks_p", 2)
        m.ps_g = banks4
        m.agg = [banks4[0:NQ, c, :] for c in range(NC)]
        m.ps_s = [banks_s[0:D, h, 0:TC * WN] for h in range(2)]
        m.ps_s2 = [banks_s[:, h, :] for h in range(2)]
        m.ps_p = [banks_p[:, h, 0:D] for h in range(2)]
        m.ps_p2 = [banks_p[0:NQ, h, :] for h in range(2)]
        m.ps_count = banks_s[0:HI, 0, 0:LO]
        m.ps_src = banks_s[0:NQ, 1, 0:NM]
        m.ps_rank = [banks4[0:EQ, b, 0:NW] for b in range(2)]
        m.ps_turn = [banks_s[:, g, 0:P] for g in range(2)]
        m.ps_deg = banks4[0:3, 0, 0:TC * WN]
        m.ps_eh = [banks_p[:, g, :] for g in range(2)]
        m.ps_degree = banks4[0:NQ, 1, 0:NC * 3 * WN]

        m.owner = sb("owner", [OQ, OC, NW])
        m.ident = sb("ident", [P, P])
        m.node1 = sb("node1", [P, WN])
        m.deg_out = sb("deg_out", [NQ, NM])
        m.deg_w, m.positive, m.inv_w, m.inv_self, m.inv_in, m.inv_out, m.stat = (
            sb(n, [NQ, NM]) for n in ("deg_w", "positive", "inv_w", "inv_self", "inv_in", "inv_out", "stat"))

        with ExitStack() as setup:
            sb = make(setup)
            m.src, m.dst = (
                sb(n, [EQ, ET], I32) for n in ("src", "dst"))
            m.tmp_i = sb("tmp_i", [EQ, ET], I32)
            m.wcol, m.win, m.whi, m.wlo, m.shi, m.slo = (
                sb(n, [EQ, ET]) for n in ("wcol", "win", "whi", "wlo", "shi", "slo"))
            m.meta = sb("meta", [EQ, ET * META])
            m.zeros = sb("zeros", [P, OQ * ROW])
            m.iota_i = sb("iota_i", [P, NW], I32)
            m.pcol_i = sb("pcol_i", [P, 1], I32)
            m.iota = sb("iota", [P, NW])
            m.iota_h = m.iota
            m.pcol = sb("pcol", [P, 1])
            m.tnum = sb("tnum", [P, 1])
            m.earlier = sb("earlier", [P, P], BF16)
            m.others = sb("others", [P, P], BF16)
            m.ones_b = sb("ones_b", [P, P], BF16)
            m.ones_f = sb("ones_f", [1, P])
            m.zero_b = sb("zero_b", [1, P], BF16)
            m.hot_hi = sb("hot_hi", [EQ, HT, HI], BF16, halves=2)
            m.hot_lo = sb("hot_lo", [EQ, HT, LO], BF16, halves=2)
            m.count = sb("count", [HI, LO])
            m.cnt, m.tiles, m.scan0, m.scan1, m.first, m.first_slot = (
                sb(n, [P, NW]) for n in ("cnt", "tiles", "scan0", "scan1", "first", "first_slot"))
            m.cnt_i = sb("cnt_i", [P, NW], I32)
            m.rows = sb("rows", [EQ, ST, ROW], halves=2)
            m.win_now = sb("win_now", [EQ, ST], halves=2)
            m.hot_shi = sb("hot_shi", [EQ, ST, NQ], BF16, halves=2)
            m.hot_slo = sb("hot_slo", [EQ, ST, NM], BF16, halves=2)
            m.ring = sb("ring", [EQ, NW], BF16, halves=4)
            m.junk = sb("junk", [EQ, NW], BF16, halves=2)
            m.slot_f = sb("slot_f", [EQ, ST], halves=2)
            m.slot_u = sb("slot_u", [EQ, ST], U32, halves=2)
            m.slot_i, m.slot_t, m.slot_p = (sb(n, [EQ, ST], I32) for n in ("slot_i", "slot_t", "slot_p"))
            m.slot_tf, m.slot_pf = (sb(n, [EQ, ST]) for n in ("slot_tf", "slot_pf"))
            prepare_edges(nc, m, src, dst, weight)
            count_windows(nc, m)
            place_windows(nc, m)
            scatter_rows(nc, m, attr)

        sb = make(whole)
        m.meta_t = sb("meta_t", [P, TP * 4])
        m.mask = sb("mask", [P, TC, WN], halves=2)
        m.eh = sb("eh_sb", [P, TC * K], halves=2)
        m.en1, m.en1_b = sb("en1", [P, 4 * K]), sb("en1_b", [P, 4 * K])
        m.x, m.h, m.y = (sb(n, [NQ, NM * D]) for n in ("x_sb", "h_sb", "y_sb"))
        m.en2, m.en2_b, m.w2 = sb("en2", [K, D, D]), sb("en2_b", [D, D]), sb("w2", [D, D])
        m.b2, m.conv_b, m.lin0_b = (sb(n, [NQ, D]) for n in ("b2", "conv_b", "lin0_b"))
        m.lin0 = sb("lin0", [P, P])
        m.gru_i, m.gru_h = sb("gru_i", [P, 4 * GATE]), sb("gru_h", [P, 4 * GATE])
        m.bias_i, m.bias_h, m.gate_b = (sb(n, [NQ, k]) for n, k in (("bias_i", 96), ("bias_h", 96), ("gate_b", GATE)))
        load_everything(nc, m, x, w)

        with ExitStack() as encode:
            sb = make(encode)
            m.rowin = sb("rowin", [P, TC * ROW], halves=2)
            m.attr = sb("attr", [P, TC * D], halves=2)
            m.attr_t = sb("attr_t", [P, P], halves=2)
            m.eh_pre = sb("eh_pre", [P, 4 * K], halves=2)
            m.deg_s = sb("deg_s", [3, TC * WN], halves=2)
            m.deg_t = sb("deg_t", [OQ, OC, 3 * WN])
            encode_edges(nc, m)
            node_degrees(nc, m)

        sb = make(whole)
        m.idx = sb("idx", [P, TC], U32, halves=2)
        m.xs = sb("xs", [P, TC * D], halves=2)
        spread, g = sb("spread", [P, 2, TC, D, WN]), sb("g", [P, 2, D, TC, WN])
        m.spread, m.g = [spread[:, h] for h in range(2)], [g[:, h] for h in range(2)]
        m.parts = spread[0:OQ].rearrange("p h t i n -> p (h t i n)").rearrange("p (ch x) -> p ch x", ch=OC)
        m.gates = g[0:NQ].rearrange("p h i t n -> p (h i t n)")
        m.s = sb("s", [D, TC * WN], halves=2)
        m.part = sb("part", [P, D], halves=2)
        m.turned_m, m.turned_h = sb("turned_m", [P, 16, NQ]), sb("turned_h", [P, 16, NQ])
        propagate(nc, m)
        convolve(nc, m)
        graph_conv(nc, m)
        self_loop_conv(nc, m)
        store_result(nc, m, out)


def kernel(x, src, dst, edge_attr_32, edge_weight, L1_gnn_lin0_w, L1_gnn_lin0_b, L1_gnn_en1_w, L1_gnn_en1_b,
           L1_gnn_en2_w, L1_gnn_en2_b, L1_gnn_conv_bias, L1_gnn_gru_wih, L1_gnn_gru_whh, L1_gnn_gru_bih,
           L1_gnn_gru_bhh, L2_gnn_weight, L2_gnn_bias):
    import numpy as np
    import concourse.bacc as bacc
    from concourse.bass_utils import run_bass_kernel_spmd

    nc = bacc.Bacc("TRN2", target_bir_lowering=False, num_devices=1)
    arrays = {}

    def put(name, a):
        arrays[name] = np.ascontiguousarray(a)
        return nc.dram_tensor(name, arrays[name].shape, mybir.dt.from_np(arrays[name].dtype), kind="ExternalInput").ap()

    t = np.transpose
    w = {
        "lin0": put("lin0_t", t(np.asarray(L1_gnn_lin0_w))), "lin0_b": put("lin0_bias", L1_gnn_lin0_b),
        "en1": put("en1_t", t(np.asarray(L1_gnn_en1_w))), "en1_b": put("en1_bias", L1_gnn_en1_b),
        "en2": put("en2_t", t(np.asarray(L1_gnn_en2_w))), "en2_b": put("en2_bias", L1_gnn_en2_b),
        "conv_b": put("conv_bias", L1_gnn_conv_bias),
        "wih": put("wih_t", t(np.asarray(L1_gnn_gru_wih))), "whh": put("whh_t", t(np.asarray(L1_gnn_gru_whh))),
        "bih": put("gru_bih", L1_gnn_gru_bih), "bhh": put("gru_bhh", L1_gnn_gru_bhh),
        "w2": put("conv2_w", L2_gnn_weight), "b2": put("conv2_bias", L2_gnn_bias),
    }
    args = [put("x", x), put("src", src), put("dst", dst), put("edge_attr", edge_attr_32), put("edge_weight", edge_weight)]
    out = nc.dram_tensor("out", (NODES, D), F32, kind="ExternalOutput").ap()
    build(nc, *args, w, out)
    return run_bass_kernel_spmd(nc, [arrays], core_ids=[0]).results[0]["out"]
```

```python
from contextlib import ExitStack, contextmanager

import concourse.bass as bass
from concourse import mybir
from concourse.alu_op_type import AluOpType as ALU

F32 = mybir.dt.float32
BF16 = mybir.dt.bfloat16
F16 = mybir.dt.float16
I32 = mybir.dt.int32
U32 = mybir.dt.uint32
ACT = mybir.ActivationFunctionType
AX = mybir.AxisListType.X

P = 128
NODES, D, EDGES, K = 6250, 32, 200000, 128
EQ, ET = 125, 1600
NQ, NM = 98, 64
WN = 16
NC = NM // WN
HI, LO = 25, 16
NW = HI * LO
TC, L, BODIES = 8, 4, 62
TP = L * TC * BODIES
OQ, OC = 124, 16
GATE = 4 * D
META = 5
ROW = META + D
STEPS0, STEPS1, ALPHA, EPS = 3, 6, 0.9, 1e-5
ST, SBODIES = 16, 50
HT, HBODIES = 40, 20
FULL = NODES // NM
REST = NODES - FULL * NM
assert EQ * ET == EDGES and TP >= EDGES // P + NW and OQ * OC == TP and NW >= NQ * NC


@contextmanager
def phase(nc, *names):
    with ExitStack() as ctx:
        sems = [ctx.enter_context(nc.semaphore(n)) for n in names]
        with nc.Block() as block:
            yield (block, *sems)
        nc.gpsimd.dma_reset()
        for s in sems:
            nc.gpsimd.sem_clear(s)
        nc.all_engine_barrier()


class Chain:

    def __init__(self, eng, sem, base=0):
        self.eng, self.sem, self.base, self.n = eng, sem, base, 0

    def __call__(self, ins):
        self.n += 1
        ins.then_inc(self.sem, 1)
        self.eng.wait_ge(self.sem, self.base + self.n)


def peeled(eng, count):
    yield 0
    with eng.Fori(1, count) as i:
        yield i


def wait_after_first(eng, sem, value):
    if not (isinstance(value, int) and value == 0):
        eng.wait_ge(sem, value)


def hold(eng, sem):
    eng.sem_inc(sem, 1)


class Mem:
    pass


def load_nodes(sp, dst, dram, sem):
    sp.dma_start(dst[0:FULL, :], dram[0:FULL * NM, :].rearrange("(q m) f -> q (m f)", m=NM)).then_inc(sem, 16)
    sp.dma_start(dst[FULL:FULL + 1, 0:REST * D],
                 dram[FULL * NM:NODES, :].rearrange("(q m) f -> q (m f)", q=1)).then_inc(sem, 16)


def prepare_edges(nc, m, src, dst, weight):
    with phase(nc, "edges_in", "prep", "iotas", "zeroed") as (block, edges_in, prep, iotas, zeroed):
        @block.sync
        def _(sp):
            sp.dma_start(m.src[:, :], src.rearrange("(q t) -> q t", t=ET)).then_inc(edges_in, 16)
            sp.dma_start(m.dst[:, :], dst.rearrange("(q t) -> q t", t=ET)).then_inc(edges_in, 16)
            sp.dma_start(m.wcol[:, :], weight.rearrange("(q t) -> q t", t=ET)).then_inc(edges_in, 16)
            sp.wait_ge(edges_in, 48)
            sp.wait_ge(zeroed, 1)
            for c in range(OC):
                sp.dma_start(m.slots.rearrange("(s t) r -> s (t r)", t=TP)[:, c * OQ * ROW:(c + 1) * OQ * ROW],
                             m.zeros[:, 0:OQ * ROW]).then_inc(edges_in, 16)
            sp.wait_ge(edges_in, 48 + 16 * OC)

        @block.gpsimd
        def _(pool):
            nc.gpsimd.iota(m.iota_i[:, :], [[1, NW]], base=0, channel_multiplier=0).then_inc(iotas, 1)
            nc.gpsimd.iota(m.pcol_i[:, :], [[1, 1]], base=0, channel_multiplier=1).then_inc(iotas, 1)

        @block.vector
        def _(dve):
            nc.vector.memset(m.zeros[:, :], 0.0).then_inc(zeroed, 1)
            do = Chain(dve, prep)
            V = nc.vector
            dve.wait_ge(iotas, 2)
            do(V.tensor_copy(m.iota[:, :], m.iota_i[:, :]))
            do(V.tensor_copy(m.iota_h[:, :], m.iota_i[:, :]))
            do(V.tensor_copy(m.pcol[:, :], m.pcol_i[:, :]))
            do(V.tensor_scalar(m.ident[:, :], m.iota[:, 0:P], m.pcol[:, 0:1], None, ALU.is_equal))
            do(V.tensor_tensor(m.fold[:, :], m.ident[:, 0:D], m.ident[:, D:2 * D], ALU.add))
            do(V.tensor_tensor(m.fold[:, :], m.fold[:, :], m.ident[:, 2 * D:3 * D], ALU.add))
            do(V.tensor_tensor(m.fold[:, :], m.fold[:, :], m.ident[:, 3 * D:4 * D], ALU.add))
            do(V.tensor_scalar(m.earlier[:, :], m.iota[:, 0:P], m.pcol[:, 0:1], None, ALU.is_gt))
            do(V.tensor_scalar(m.others[:, :], m.iota[:, 0:P], m.pcol[:, 0:1], None, ALU.is_le))
            do(V.memset(m.ones_b[:, :], 1.0))
            do(V.memset(m.ones_f[:, :], 1.0))
            do(V.memset(m.zero_b[:, :], 0.0))
            do(V.tensor_scalar_add(m.node1[:, :], m.iota[:, 0:WN], 1.0))
            dve.wait_ge(edges_in, 48)
            meta_i = m.meta.bitcast(I32).rearrange("q (t r) -> q t r", r=META)
            meta_f = m.meta.rearrange("q (t r) -> q t r", r=META)
            do(V.tensor_copy(meta_i[:, :, 0], m.src[:, :]))
            do(V.tensor_scalar(m.tmp_i[:, :], m.dst[:, :], WN - 1, None, ALU.bitwise_and))
            do(V.tensor_scalar_add(meta_f[:, :, 1], m.tmp_i[:, :], 1.0))
            do(V.tensor_copy(meta_f[:, :, 2], m.wcol[:, :]))
            do(V.tensor_tensor(meta_f[:, :, 3], m.src[:, :], m.dst[:, :], ALU.not_equal))
            do(V.memset(meta_f[:, :, 4], 1.0))
            for out, x, shift, mask in ((m.win, m.dst, 4, 0xffff), (m.whi, m.dst, 8, 0xffff), (m.wlo, m.dst, 4, 15),
                                        (m.shi, m.src, 6, 0xffff), (m.slo, m.src, 0, 63)):
                do(V.tensor_scalar(m.tmp_i[:, :], x[:, :], shift, mask, ALU.logical_shift_right, ALU.bitwise_and))
                do(V.tensor_copy(out[:, :], m.tmp_i[:, :]))


def onehots(nc, out, digit, iota, n, w):
    return nc.vector.tensor_tensor(out, digit.unsqueeze(2).broadcast_to([EQ, n, w]),
                                   iota[0:EQ, 0:w].unsqueeze(1).broadcast_to([EQ, n, w]), ALU.is_equal)


def count_windows(nc, m):
    with phase(nc, "hots", "counted", "stored") as (block, hots, counted, stored):
        @block.vector
        def _(dve):
            with dve.Fori(0, HBODIES) as i:
                for h in range(2):
                    dve.wait_ge(counted, i * 2 + h + 1)
                    c = bass.ds(i * 2 * HT + h * HT, HT)
                    onehots(nc, m.hot_hi[h], m.whi[:, c], m.iota, HT, HI).then_inc(hots, 1)
                    onehots(nc, m.hot_lo[h], m.wlo[:, c], m.iota, HT, LO).then_inc(hots, 1)
            dve.wait_ge(counted, 2 * HBODIES + 3)
            nc.vector.tensor_copy(m.count[:, :], m.ps_count).then_inc(hots, 1)

        @block.tensor
        def _(pe):
            nc.tensor.matmul(m.ps_count, m.zero_b[0:1, 0:HI], m.zero_b[0:1, 0:LO],
                             start=True, stop=False, skip_group_check=True).then_inc(counted, 2)
            with pe.Fori(0, HBODIES) as i:
                for h in range(2):
                    pe.wait_ge(hots, i * 4 + h * 2 + 2)
                    for t in range(HT):
                        mm = nc.tensor.matmul(m.ps_count, m.hot_hi[h][:, t, :], m.hot_lo[h][:, t, :],
                                              start=False, stop=False, skip_group_check=True)
                    mm.then_inc(counted, 1)
            nc.tensor.matmul(m.ps_count, m.zero_b[0:1, 0:HI], m.zero_b[0:1, 0:LO], start=False, stop=True,
                             skip_group_check=True).then_inc(counted, 1)

        @block.sync
        def _(sp):
            sp.wait_ge(hots, 4 * HBODIES + 1)
            sp.dma_start(m.row_dram.rearrange("(h l) -> h l", l=LO), m.count[:, :]).then_inc(stored, 16)
            sp.wait_ge(stored, 16)
            sp.dma_start(m.cnt[:, :], m.row_dram.unsqueeze(0).broadcast_to([P, NW])).then_inc(stored, 16)
            sp.wait_ge(stored, 32)


def place_windows(nc, m):
    with phase(nc, "placed") as (block, placed):
        @block.vector
        def _(dve):
            do = Chain(dve, placed)
            V = nc.vector
            do(V.tensor_scalar_add(m.cnt[:, :], m.cnt[:, :], float(P - 1)))
            do(V.tensor_copy(m.cnt_i[:, :], m.cnt[:, :]))
            do(V.tensor_scalar(m.cnt_i[:, :], m.cnt_i[:, :], 7, None, ALU.logical_shift_right))
            do(V.tensor_copy(m.tiles[:, :], m.cnt_i[:, :]))
            do(V.tensor_scalar_max(m.tiles[:, :], m.tiles[:, :], 1.0))
            a, b = m.tiles, m.scan0
            shift = 1
            while shift < NW:
                do(V.tensor_copy(b[:, 0:shift], a[:, 0:shift]))
                do(V.tensor_tensor(b[:, shift:NW], a[:, shift:NW], a[:, 0:NW - shift], ALU.add))
                a, b = b, (m.scan1 if b is m.scan0 else m.scan0)
                shift *= 2
            do(V.tensor_tensor(m.first[:, :], a[:, :], m.tiles[:, :], ALU.subtract))
            do(V.tensor_scalar_mul(m.first_slot[:, :], m.first[:, :], float(P)))
            for c in range(OC):
                do(V.tensor_scalar_add(m.tnum[:, :], m.pcol[:, :], float(OQ * c)))
                do(V.tensor_scalar(b[0:OQ, :], m.first[0:OQ, :], m.tnum[0:OQ, 0:1], None, ALU.is_le))
                do(V.scalar_tensor_tensor(m.owner[:, c, :], a[0:OQ, :], m.tnum[0:OQ, 0:1], b[0:OQ, :],
                                          ALU.is_gt, ALU.mult))


def scatter_rows(nc, m, attr):
    attr_v = attr.rearrange("(q t) f -> q t f", t=ET)
    with phase(nc, "hot_ready", "ranked", "slot_read", "row_meta", "srchot", "srccount",
               "attr_a", "attr_b", "scat_a", "scat_b", "own", "held_sp", "held_pool") as (
            block, hot_ready, ranked, slot_read, row_meta, srchot, srccount, attr_a, attr_b, scat_a, scat_b, own,
            held_sp, held_pool):
        attr_in, scattered = (attr_a, attr_b), (scat_a, scat_b)

        @block.sync
        def _(sp):
            for i in peeled(sp, SBODIES):
                for h in range(2):
                    wait_after_first(sp, scattered[h], i * 16 * ST)
                    hold(sp, held_sp)
                    sp.dma_start(m.rows[h][:, :, META:ROW],
                                 attr_v[:, bass.ds(i * 2 * ST + h * ST, ST), :]).then_inc(attr_in[h], 16)

        @block.gpsimd
        def _(pool):
            with pool.Fori(0, SBODIES) as i:
                for h in range(2):
                    pool.wait_ge(row_meta, i * 2 + h + 1)
                    pool.wait_ge(attr_in[h], i * 16 + 16)
                    hold(pool, held_pool)
                    for t in range(ST):
                        nc.gpsimd.indirect_dma_start(
                            m.slots, bass.IndirectOffsetOnAxis(ap=m.slot_u[h][:, t:t + 1], axis=0),
                            m.rows[h][:, t, :], None).then_inc(scattered[h], 16)
            for h in range(2):
                pool.wait_ge(scattered[h], SBODIES * 16 * ST)

        @block.vector
        def _(dve):
            V = nc.vector
            chain = 8
            V.memset(m.ring[2], 0.0).then_inc(own, 1)
            V.memset(m.ring[3], 0.0).then_inc(hot_ready, 1)
            dve.wait_ge(own, 1)
            dve.wait_ge(hot_ready, 1)
            dve.sem_inc(slot_read, 2)
            for i in peeled(dve, SBODIES):
                for h in range(2):
                    do = Chain(dve, own, 1 + i * 2 * chain + h * chain)
                    c = bass.ds(i * 2 * ST + h * ST, ST)
                    do(V.tensor_copy(m.win_now[h], m.win[:, c]))
                    dve.wait_ge(srccount, i * 2 + h + 1)
                    onehots(nc, m.hot_shi[h], m.shi[:, c], m.iota, ST, NQ).then_inc(srchot, 1)
                    onehots(nc, m.hot_slo[h], m.slo[:, c], m.iota, ST, NM).then_inc(srchot, 1)

                    def hot(t):
                        V.tensor_scalar(m.ring[(h * ST + t) % 4], m.iota_h[0:EQ, :], m.win_now[h][:, t:t + 1], None,
                                        ALU.is_equal).then_inc(hot_ready, 1)

                    hot(0)
                    for t in range(ST):
                        if t + 1 < ST:
                            hot(t + 1)
                        n = i * 2 * ST + h * ST + t
                        dve.wait_ge(ranked, n + 1)
                        ins = V.tensor_tensor_reduce(
                            out=m.junk[t % 2], in0=m.ring[(h * ST + t) % 4], in1=m.ps_rank[t % 2],
                            scale=1.0, scalar=0.0, op0=ALU.mult, op1=ALU.add, accum_out=m.slot_f[h][:, t:t + 1])
                        ins.then_inc(slot_read, 1)
                    dve.wait_ge(slot_read, i * 2 * ST + h * ST + ST + 2)
                    do(V.tensor_copy(m.slot_i, m.slot_f[h]))
                    do(V.tensor_scalar(m.slot_t, m.slot_i, 7, None, ALU.logical_shift_right))
                    do(V.tensor_scalar(m.slot_p, m.slot_i, P - 1, None, ALU.bitwise_and))
                    do(V.tensor_copy(m.slot_tf, m.slot_t))
                    do(V.tensor_copy(m.slot_pf, m.slot_p))
                    wait_after_first(dve, scattered[h], i * 16 * ST)
                    do(V.scalar_tensor_tensor(m.slot_u[h], m.slot_pf, float(TP), m.slot_tf, ALU.mult, ALU.add))
                    do(V.tensor_copy(m.rows[h][:, :, 0:META],
                                     m.meta[:, bass.ds((i * 2 * ST + h * ST) * META, ST * META)]
                                     .rearrange("q (t r) -> q t r", r=META)))
                    dve.sem_inc(row_meta, 1)
                    assert do.n == chain
            dve.wait_ge(srccount, 2 * SBODIES + 3)
            V.tensor_copy(m.deg_out[:, :], m.ps_src).then_inc(own, 1)

        @block.tensor
        def _(pe):
            mm = nc.tensor.matmul
            for b in range(2):
                mm(m.ps_rank[b], m.ones_f[0:1, 0:EQ], m.first_slot[0:1, :], start=True, stop=False,
                   skip_group_check=True)
            mm(m.ps_src, m.zero_b[0:1, 0:NQ], m.zero_b[0:1, 0:NM], start=True, stop=False,
               skip_group_check=True).then_inc(srccount, 2)
            with pe.Fori(0, SBODIES) as i:
                for h in range(2):
                    pe.wait_ge(srchot, i * 4 + h * 2 + 2)
                    for t in range(ST):
                        s = mm(m.ps_src, m.hot_shi[h][:, t, :], m.hot_slo[h][:, t, :], start=False, stop=False,
                               skip_group_check=True)
                    s.then_inc(srccount, 1)
                    for t in range(ST):
                        n = i * 2 * ST + h * ST + t
                        now, r = m.ps_rank[t % 2], h * ST + t
                        pe.wait_ge(hot_ready, n + 2)
                        pe.wait_ge(slot_read, n + 1)
                        mm(now, m.others[0:EQ, 0:EQ], m.ring[(r + 2) % 4], start=False, stop=False,
                           skip_group_check=True)
                        mm(now, m.ones_b[0:EQ, 0:EQ], m.ring[(r + 3) % 4], start=False, stop=False,
                           skip_group_check=True)
                        mm(now, m.earlier[0:EQ, 0:EQ], m.ring[r % 4], start=False, stop=True,
                           skip_group_check=True).then_inc(ranked, 1)
            mm(m.ps_src, m.zero_b[0:1, 0:NQ], m.zero_b[0:1, 0:NM], start=False, stop=True,
               skip_group_check=True).then_inc(srccount, 1)


def encode_edges(nc, m):
    slots_v = m.slots.rearrange("(s t) r -> s (t r)", t=TP)
    with phase(nc, "rows_a", "rows_b", "rows_c", "rows_d", "meta_kept", "masked", "degs", "turned", "turned_sb",
               "eh_ps", "biased", "relu", "eh_out_a", "eh_out_b", "eh_out_c", "eh_out_d", "deg_sb",
               "deg_out_a", "deg_out_b", "deg_out_c", "deg_out_d", "held_sp") as (block, *sems):
        rows_in, (meta_kept, masked, degs, turned, turned_sb, eh_ps, biased, relu) = sems[0:4], sems[4:12]
        eh_out, deg_sb, deg_out, held_sp = sems[12:16], sems[16], sems[17:21], sems[21]

        def staged(i, first, second):
            for h in range(L):
                if h == 0:
                    first(i, 0)
                if h + 1 < L:
                    first(i, h + 1)
                second(i, h)

        @block.sync
        def _(sp):
            with sp.Fori(0, BODIES) as i:
                for h in range(L):
                    n = i * L + h
                    sp.wait_ge(meta_kept, n * 2 + 2)
                    hold(sp, held_sp)
                    sp.wait_ge(degs, n + 1)
                    hold(sp, held_sp)
                    sp.dma_start(m.rowin[h], slots_v[:, bass.ds(n * TC * ROW, TC * ROW)]).then_inc(rows_in[h], 16)

        @block.vector
        def _(dve):
            V = nc.vector
            dve.sem_inc(meta_kept, 2 * L)
            dve.sem_inc(biased, 2)

            def unpack(i, h):
                n = i * L + h
                dve.wait_ge(rows_in[h], i * 16 + 16)
                rows = m.rowin[h].rearrange("s (t r) -> s t r", r=ROW)
                V.tensor_copy(m.src_t[:, bass.ds(n * TC, TC)].bitcast(F32), rows[:, :, 0])
                V.tensor_copy(m.meta_t[:, bass.ds(n * TC * 3, TC * 3)].rearrange("s (t r) -> s t r", r=3),
                              rows[:, :, 1:4]).then_inc(meta_kept, 1)
                dve.wait_ge(turned, n * 2 + 2)
                V.tensor_copy(m.attr[h % 2].rearrange("s (t f) -> s t f", f=D),
                              rows[:, :, META:ROW]).then_inc(meta_kept, 1)
                dve.wait_ge(degs, n + 1)
                V.tensor_tensor(m.mask[h], rows[:, :, 1].unsqueeze(2).broadcast_to([P, TC, WN]),
                                m.node1[:, :].unsqueeze(1).broadcast_to([P, TC, WN]),
                                ALU.is_equal).then_inc(masked, 1)

            def bias(i, h):
                n = i * L + h
                for g in range(2):
                    dve.wait_ge(eh_ps, n * 2 + g + 5)
                    dve.wait_ge(relu, n * 2 + g + 1)
                    V.tensor_tensor(m.eh_pre[g], m.ps_eh[g], m.en1_b[:, :], ALU.add).then_inc(biased, 1)

            with dve.Fori(0, BODIES) as i:
                staged(i, unpack, bias)

        @block.tensor
        def _(pe):
            pe.sem_inc(degs, L)
            pe.sem_inc(turned, 4)
            pe.sem_inc(eh_ps, 4)

            def turn_and_sum(i, h):
                n = i * L + h
                rows = m.rowin[h].rearrange("s (t r) -> s t r", r=ROW)
                pe.wait_ge(rows_in[h], i * 16 + 16)
                pe.wait_ge(meta_kept, n * 2 + 2 + 2 * L)
                for g in range(2):
                    pe.wait_ge(turned_sb, n * 2 + g + 1)
                    nc.tensor.transpose(m.ps_turn[g], m.attr[h % 2][:, g * P:(g + 1) * P],
                                        m.ident[:, :]).then_inc(turned, 1)
                pe.wait_ge(masked, n + 1)
                pe.wait_ge(deg_sb, n + 1)
                for t in range(TC):
                    s = nc.tensor.matmul(m.ps_deg[:, t * WN:(t + 1) * WN], rows[:, t, 2:META],
                                         m.mask[h][:, t, :], start=True, stop=True)
                s.then_inc(degs, 1)

            def encode(i, h):
                n = i * L + h
                for g in range(2):
                    pe.wait_ge(turned_sb, n * 2 + g + 3)
                    pe.wait_ge(biased, n * 2 + g + 1)
                    nc.tensor.matmul(m.ps_eh[g], m.attr_t[2 * (h % 2) + g], m.en1[:, :], start=True,
                                     stop=True).then_inc(eh_ps, 1)

            with pe.Fori(0, BODIES) as i:
                staged(i, turn_and_sum, encode)

        @block.scalar
        def _(act):
            act.sem_inc(turned_sb, 2)
            act.sem_inc(relu, 2)
            act.sem_inc(deg_sb, 1)

            def copies(i, h):
                n = i * L + h
                for g in range(2):
                    act.wait_ge(turned, n * 2 + g + 5)
                    act.wait_ge(eh_ps, n * 2 + g + 1)
                    nc.scalar.activation(m.attr_t[2 * (h % 2) + g], m.ps_turn[g], ACT.Copy).then_inc(turned_sb, 1)
                act.wait_ge(degs, n + 1 + L)
                wait_after_first(act, deg_out[h], i * 16)
                nc.scalar.activation(m.deg_s[h], m.ps_deg, ACT.Copy).then_inc(deg_sb, 1)
                act.wait_ge(deg_sb, n + 2)
                act.dma_start(m.deg_dram[:, bass.ds(n * TC * WN, TC * WN)], m.deg_s[h]).then_inc(deg_out[h], 16)

            def rectify(i, h):
                n = i * L + h
                wait_after_first(act, eh_out[h], i * 16)
                for g in range(2):
                    act.wait_ge(biased, n * 2 + g + 3)
                    nc.scalar.activation(m.eh[h][:, g * 4 * K:(g + 1) * 4 * K], m.eh_pre[g],
                                         ACT.Relu).then_inc(relu, 1)
                act.wait_ge(relu, n * 2 + 4)
                act.dma_start(m.eh_dram[:, bass.ds(n * TC * K, TC * K)], m.eh[h]).then_inc(eh_out[h], 16)

            for i in peeled(act, BODIES):
                staged(i, copies, rectify)
            for h in range(L):
                act.wait_ge(eh_out[h], BODIES * 16)
                act.wait_ge(deg_out[h], BODIES * 16)


def owner_of(m, ch, c):
    return m.owner[:, ch, 0:NQ * NC].rearrange("t (q c) -> t c q", c=NC)[:, c, :]


def node_degrees(nc, m):
    with phase(nc, "deg_in", "summed", "copied", "rooted", "own") as (block, deg_in, summed, copied, rooted, own):
        @block.sync
        def _(sp):
            for j in range(3):
                sp.dma_start(m.deg_t[:, :, j * WN:(j + 1) * WN],
                             m.deg_dram[j, :].rearrange("(ch t n) -> t ch n", t=OQ, n=WN)).then_inc(deg_in, 16)

        @block.tensor
        def _(pe):
            pe.wait_ge(deg_in, 48)
            for c in range(NC):
                for ch in range(OC):
                    mm = nc.tensor.matmul(m.ps_degree[:, c * 3 * WN:(c + 1) * 3 * WN], owner_of(m, ch, c),
                                          m.deg_t[:, ch, :], start=(ch == 0), stop=(ch == OC - 1))
            mm.then_inc(summed, 1)

        @block.vector
        def _(dve):
            V = nc.vector
            do = Chain(dve, own)
            dve.wait_ge(summed, 1)
            psd = m.ps_degree.rearrange("q (c j n) -> q c j n", c=NC, j=3)
            per = lambda x: x.rearrange("q (c n) -> q c n", c=NC)
            do(V.tensor_copy(per(m.deg_w), psd[:, :, 0, :]))
            do(V.tensor_scalar(m.positive, m.deg_w, 0.0, 2.0 ** 15, ALU.is_gt, ALU.mult))
            do(V.tensor_scalar_max(m.deg_w, m.deg_w, 1e-38))
            do(V.tensor_scalar_add(per(m.inv_self), psd[:, :, 1, :], 1.0))
            do(V.tensor_scalar_max(per(m.inv_in), psd[:, :, 2, :], 1.0))
            do(V.tensor_scalar_max(m.inv_out, m.deg_out[:, :], 1.0))
            dve.sem_inc(copied, 1)
            dve.wait_ge(rooted, 4)
            for x in (m.deg_w, m.inv_self, m.inv_in, m.inv_out):
                do(V.reciprocal(x, x))
            do(V.tensor_tensor(m.inv_w, m.deg_w, m.positive, ALU.mult))

        @block.scalar
        def _(act):
            act.wait_ge(copied, 1)
            nc.scalar.activation(m.deg_w, m.deg_w, ACT.Sqrt, scale=2.0 ** 30).then_inc(rooted, 1)
            for x in (m.inv_self, m.inv_in, m.inv_out):
                nc.scalar.activation(x, x, ACT.Sqrt).then_inc(rooted, 1)


def edge_pass(nc, m, weight, after, edge_matrices=False):
    per = 2 if weight is not None else 1
    GT = 16 * TC
    with phase(nc, "idx_a", "idx_b", "idx_c", "idx_d", "gath_a", "gath_b", "gath_c", "gath_d",
               "eh_a", "eh_b", "eh_c", "eh_d", "st_a", "st_b", "st_c", "st_d", "masked", "made", "summed",
               "g_done", "g_sb", "s_sb", "grouped", "pj_sb", "folded", "out_sb", "held_sp", "held_pool") as (
            block, *sems):
        idx_in, gathered, eh_in, stored = sems[0:4], sems[4:8], sems[8:12], sems[12:16]
        masked, made, summed, g_done, g_sb, s_sb, grouped, pj_sb, folded, out_sb, held_sp, held_pool = sems[16:28]

        @block.gpsimd
        def _(pool):
            with pool.Fori(0, BODIES) as i:
                for h in range(L):
                    n = i * L + h
                    pool.wait_ge(idx_in[h], i * 16 + 16)
                    pool.wait_ge(summed, n + 1)
                    if edge_matrices:
                        pool.wait_ge(made, n + 1)
                    hold(pool, held_pool)
                    for t in range(TC):
                        nc.gpsimd.indirect_dma_start(
                            m.xs[h][:, t * D:(t + 1) * D], None, m.node_dram,
                            bass.IndirectOffsetOnAxis(ap=m.idx[h][:, t:t + 1], axis=0)).then_inc(gathered[h], 16)
            for h in range(L):
                pool.wait_ge(gathered[h], BODIES * GT)

        @block.sync
        def _(sp):
            for i in peeled(sp, BODIES):
                for h in range(L):
                    n = i * L + h
                    wait_after_first(sp, gathered[h], i * GT)
                    hold(sp, held_sp)
                    sp.dma_start(m.idx[h], m.src_t[:, bass.ds(n * TC, TC)]).then_inc(idx_in[h], 16)
                    if edge_matrices:
                        sp.wait_ge(g_done, n * TC + TC)
                        hold(sp, held_sp)
                        sp.dma_start(m.eh[h], m.eh_dram[:, bass.ds(n * TC * K, TC * K)]).then_inc(eh_in[h], 16)

        @block.vector
        def _(dve):
            V = nc.vector
            if edge_matrices:
                dve.sem_inc(made, L)

            def meta(n, word):
                return m.meta_t[:, bass.ds(n * TC * 3, TC * 3)].rearrange("s (t r) -> s t r", r=3)[:, :, word]

            with dve.Fori(0, BODIES) as i:
                for h in range(L):
                    n = i * L + h
                    dve.wait_ge(summed, n + 1)
                    if edge_matrices:
                        dve.wait_ge(made, n + 1)
                    V.tensor_tensor(m.mask[h], meta(n, 0).unsqueeze(2).broadcast_to([P, TC, WN]),
                                    m.node1[:, :].unsqueeze(1).broadcast_to([P, TC, WN]),
                                    ALU.is_equal).then_inc(masked, 1)
                    if weight is not None:
                        dve.wait_ge(masked, n * 2 + 1)
                        V.tensor_tensor(m.mask[h], m.mask[h], meta(n, weight).unsqueeze(2).broadcast_to([P, TC, WN]),
                                        ALU.mult).then_inc(masked, 1)
                    if edge_matrices:
                        dve.wait_ge(masked, n + 1)
                        dve.wait_ge(gathered[h], i * GT + GT)
                        dve.wait_ge(g_done, (n - 1 + L) * TC)
                        V.tensor_tensor(
                            m.spread[h % 2],
                            m.xs[h].rearrange("s (t i) -> s t i", i=D).unsqueeze(3).broadcast_to([P, TC, D, WN]),
                            m.mask[h].unsqueeze(2).broadcast_to([P, TC, D, WN]), ALU.mult).then_inc(made, 1)

        @block.tensor
        def _(pe):
            mm = nc.tensor.matmul
            pe.sem_inc(summed, L)
            pe.sem_inc(folded, 2)
            if edge_matrices:
                pe.sem_inc(grouped, 2)
                pe.sem_inc(g_done, L * TC)

            def sum_rows(i, h):
                n = i * L + h
                pe.wait_ge(gathered[h], i * GT + GT)
                pe.wait_ge(masked, n * per + per)
                pe.wait_ge(s_sb, n + 1)
                for t in range(TC):
                    s = mm(m.ps_s[:, t * WN:(t + 1) * WN], m.xs[h][:, t * D:(t + 1) * D],
                           m.mask[h][:, t, :], start=True, stop=True)
                s.then_inc(summed, 1)

            def outer(i, h):
                n = i * L + h
                pe.wait_ge(eh_in[h], i * 16 + 16)
                pe.wait_ge(made, n + 1 + L)
                for t in range(TC):
                    pe.wait_ge(g_sb, n * TC + t + 1)
                    mm(m.ps_g[:, t % 4, :], m.eh[h][:, t * K:(t + 1) * K], m.spread[h % 2][:, t, :, :],
                       start=True, stop=True).then_inc(g_done, 1)

            def group(i, h):
                n = i * L + h
                pe.wait_ge(s_sb, n + 2)
                pe.wait_ge(g_sb, n * TC + TC + 4)
                pe.wait_ge(pj_sb, n + 1)
                out = m.ps_pj[h % 2]
                for d in range(D // 4):
                    for j in range(4):
                        last = d == D // 4 - 1 and j > 0
                        mm(out[D * j:D * (j + 1), :], m.en2[:, 4 * d + j, :],
                           m.g[h % 2][:, 4 * d + j, :, :], start=(d == 0), stop=last)
                mm(out[0:D, :], after, m.s[h % 2], start=False, stop=True).then_inc(grouped, 1)

            def fold(i, h):
                n = i * L + h
                pe.wait_ge(pj_sb, n + 3)
                pe.wait_ge(out_sb, n + 1)
                mm(m.ps_out, m.pj[h % 2], m.fold, start=True, stop=True).then_inc(folded, 1)

            def project(i, h):
                n = i * L + h
                pe.wait_ge(s_sb, n + 2)
                pe.wait_ge(out_sb, n + 1)
                mm(m.ps_out, m.s[h % 2], after, start=True, stop=True).then_inc(folded, 1)

            with pe.Fori(0, BODIES) as i:
                for h in range(L):
                    sum_rows(i, h)
                    if edge_matrices:
                        outer(i, h)
                        if h >= 1:
                            group(i, h - 1)
                        if h >= 2:
                            fold(i, h - 2)
                    else:
                        project(i, h)
                if edge_matrices:
                    group(i, L - 1)
                    fold(i, L - 2)
                    fold(i, L - 1)

        @block.scalar
        def _(act):
            copy = ACT.Copy
            act.sem_inc(s_sb, 1)
            act.sem_inc(out_sb, 1)
            if edge_matrices:
                act.sem_inc(g_sb, 4)
                act.sem_inc(pj_sb, 2)

            def copy_sums(i, h):
                n = i * L + h
                act.wait_ge(summed, n + 1 + L)
                act.wait_ge(grouped if edge_matrices else folded, n + 1)
                nc.scalar.activation(m.s[h % 2], m.ps_s, copy).then_inc(s_sb, 1)

            def copy_outer(i, h):
                n = i * L + h
                for t in range(TC):
                    act.wait_ge(g_done, (n + L) * TC + t + 1)
                    nc.scalar.activation(m.g[h % 2][:, :, t, :],
                                         m.ps_g[:, t % 4, :].rearrange("k (i n) -> k i n", n=WN), copy).then_inc(g_sb, 1)

            def copy_groups(i, h):
                n = i * L + h
                act.wait_ge(grouped, n + 3)
                act.wait_ge(folded, n + 1)
                nc.scalar.activation(m.pj[h % 2], m.ps_pj[h % 2], copy).then_inc(pj_sb, 1)

            def store(i, h):
                n = i * L + h
                act.wait_ge(folded, n + 3)
                wait_after_first(act, stored[h], i * 16)
                nc.scalar.activation(m.part[h], m.ps_out, copy).then_inc(out_sb, 1)
                act.wait_ge(out_sb, n + 2)
                act.dma_start(m.part_dram[bass.ds(n * TC * WN, TC * WN), :], m.part[h]).then_inc(stored[h], 16)

            for i in peeled(act, BODIES):
                for h in range(L):
                    copy_sums(i, h)
                    if edge_matrices:
                        copy_outer(i, h)
                        if h >= 1:
                            copy_groups(i, h - 1)
                        if h >= 2:
                            store(i, h - 2)
                    else:
                        store(i, h)
                if edge_matrices:
                    copy_groups(i, L - 1)
                    store(i, L - 2)
                    store(i, L - 1)
            for h in range(L):
                act.wait_ge(stored[h], BODIES * 16)


def add_tiles(nc, m):
    with phase(nc, "parts_in", "agg") as (block, parts_in, agg):
        @block.sync
        def _(sp):
            parts = m.part_dram.rearrange("(ch t n) o -> t ch (n o)", t=OQ, n=WN)
            sp.dma_start(m.parts, parts).then_inc(parts_in, 16)
            sp.wait_ge(parts_in, 16)

        @block.tensor
        def _(pe):
            pe.wait_ge(parts_in, 16)
            for c in range(NC):
                for ch in range(OC):
                    mm = nc.tensor.matmul(m.agg[c], owner_of(m, ch, c), m.parts[:, ch, :],
                                          start=(ch == 0), stop=(ch == OC - 1))
            mm.then_inc(agg, 1)
            pe.wait_ge(agg, 1)


def by_node(x, rows=NM):
    return x.unsqueeze(2).broadcast_to([NQ, rows, D])


def by_feature(x, rows=NM):
    return x[:, 0:D].unsqueeze(1).broadcast_to([NQ, rows, D])


def feats(x):
    return x.rearrange("q (m f) -> q m f", f=D)


def layer_norm(nc, m, do, to_act, from_act, x, y):
    V = nc.vector
    do(V.tensor_tensor(x, x, y, ALU.add))
    do(V.tensor_reduce(m.stat, feats(x), AX, ALU.add))
    do(V.tensor_scalar_mul(m.stat, m.stat, 1.0 / D))
    do(V.tensor_tensor(feats(x), feats(x), by_node(m.stat), ALU.subtract))
    do(V.tensor_tensor(y, x, x, ALU.mult))
    do(V.tensor_reduce(m.stat, feats(y), AX, ALU.add))
    do(V.tensor_scalar(m.stat, m.stat, 1.0 / D, EPS, ALU.mult, ALU.add))
    do.eng.sem_inc(to_act, 1)
    do.eng.wait_ge(from_act, 1)
    do(V.reciprocal(m.stat, m.stat))
    do(V.tensor_tensor(feats(x), feats(x), by_node(m.stat), ALU.mult))


def root_for_norm(nc, m, act, to_act, from_act):
    act.wait_ge(to_act, 1)
    nc.scalar.activation(m.stat, m.stat, ACT.Sqrt).then_inc(from_act, 1)


def store_nodes(sp, m, x, ready, sem):
    sp.wait_ge(ready, 1)
    sp.dma_start(m.node_dram.rearrange("(q m) f -> q (m f)", m=NM), x).then_inc(sem, 16)
    sp.wait_ge(sem, 16)


def load_everything(nc, m, x, w):
    with phase(nc, "cleared", "loaded") as (block, cleared, loaded):
        @block.vector
        def _(dve):
            do = Chain(dve, cleared)
            for t in (m.x, m.en1, m.lin0, m.gru_i, m.gru_h):
                do(nc.vector.memset(t, 0.0))

        @block.sync
        def _(sp):
            sp.wait_ge(cleared, 5)
            n = 0

            def load(out, in_):
                nonlocal n
                sp.dma_start(out, in_).then_inc(loaded, 16)
                n += 16

            def spread(x, rows, times):
                return x.unsqueeze(0).unsqueeze(0).broadcast_to([rows, times, x.shape[0]])

            load_nodes(sp, m.x, x, loaded)
            n += 32
            load(m.en2.rearrange("k i o -> k (i o)"), w["en2"])
            load(m.en2_b, w["en2_b"].rearrange("(i o) -> i o", o=D))
            load(m.w2, w["w2"])
            load(m.b2, w["b2"].unsqueeze(0).broadcast_to([NQ, D]))
            load(m.conv_b, w["conv_b"].unsqueeze(0).broadcast_to([NQ, D]))
            load(m.lin0_b, w["lin0_b"].unsqueeze(0).broadcast_to([NQ, D]))
            load(m.en1_b.rearrange("p (j k) -> p j k", k=K), spread(w["en1_b"], P, 4))
            for dst, src, a, b in ((m.bias_i, "bih", 0, 2 * D), (m.bias_h, "bhh", 0, 2 * D)):
                load(dst, w[src].unsqueeze(0).broadcast_to([NQ, 3 * D]))
            for j in range(4):
                rows = slice(D * j, D * (j + 1))
                load(m.en1[rows, j * K:(j + 1) * K], w["en1"])
                load(m.lin0[rows, j * D:(j + 1) * D], w["lin0"])
                load(m.gru_i[rows, j * GATE:j * GATE + 3 * D], w["wih"])
                load(m.gru_h[rows, j * GATE:j * GATE + 2 * D], w["whh"][:, 0:2 * D])
                load(m.gru_h[rows, j * GATE + 3 * D:(j + 1) * GATE], w["whh"][:, 2 * D:3 * D])
            sp.wait_ge(loaded, n)
    with phase(nc, "own") as (block, own):
        @block.vector
        def _(dve):
            do = Chain(dve, own)
            V = nc.vector
            do(V.tensor_tensor(m.gate_b[:, 0:2 * D], m.bias_i[:, 0:2 * D], m.bias_h[:, 0:2 * D], ALU.add))
            do(V.tensor_copy(m.gate_b[:, 2 * D:3 * D], m.bias_i[:, 2 * D:3 * D]))
            do(V.tensor_copy(m.gate_b[:, 3 * D:GATE], m.bias_h[:, 2 * D:3 * D]))


def propagate(nc, m):
    def scaled_state(src):
        with phase(nc, "ready", "stored", "own") as (block, ready, stored, own):
            @block.vector
            def _(dve):
                do = Chain(dve, own)
                do(nc.vector.tensor_tensor(feats(m.y), feats(src), by_node(m.inv_w), ALU.mult))
                dve.sem_inc(ready, 1)

            @block.sync
            def _(sp):
                store_nodes(sp, m, m.y, ready, stored)

    scaled_state(m.x)
    with nc.Fori(0, STEPS0):
        edge_pass(nc, m, 1, m.ident[0:D, 0:D])
        add_tiles(nc, m)
        with phase(nc, "ready", "stored", "own") as (block, ready, stored, own):
            @block.vector
            def _(dve):
                V = nc.vector
                do = Chain(dve, own)
                do(V.tensor_scalar_mul(m.y, m.x, 1.0 - ALPHA))
                for c in range(NC):
                    part = slice(c * WN * D, (c + 1) * WN * D)
                    do(V.tensor_tensor(feats(m.h[:, part]), feats(m.agg[c]),
                                       by_node(m.inv_w[:, c * WN:(c + 1) * WN], WN), ALU.mult))
                do(V.scalar_tensor_tensor(m.h, m.h, ALPHA, m.y, ALU.mult, ALU.add))
                do(V.tensor_scalar(m.h, m.h, 0.0, 1.0, ALU.max, ALU.min))
                do(V.tensor_tensor(feats(m.y), feats(m.h), by_node(m.inv_w), ALU.mult))
                dve.sem_inc(ready, 1)

            @block.sync
            def _(sp):
                store_nodes(sp, m, m.y, ready, stored)
    norm_phase(nc, m)


def norm_phase(nc, m):
    with phase(nc, "to_act", "from_act", "own") as (block, to_act, from_act, own):
        @block.vector
        def _(dve):
            layer_norm(nc, m, Chain(dve, own), to_act, from_act, m.x, m.h)

        @block.scalar
        def _(act):
            root_for_norm(nc, m, act, to_act, from_act)


def turn(nc, m, pe, x, out_i, turned, turned_sb):
    for c in range(NC):
        s = out_i * NC + c
        if s >= 2:
            pe.wait_ge(turned_sb, s - 1)
        for j in range(4):
            mm = nc.tensor.transpose(m.ps_s2[s % 2][:, j * NQ:(j + 1) * NQ], x[:, (4 * c + j) * P:(4 * c + j + 1) * P],
                                     m.ident[0:NQ, 0:NQ])
        mm.then_inc(turned, 1)


def copy_turned(nc, m, act, out, out_i, turned, turned_sb):
    for c in range(NC):
        s = out_i * NC + c
        act.wait_ge(turned, s + 1)
        nc.scalar.activation(out[:, 4 * c:4 * c + 4, :], m.ps_s2[s % 2][:, 0:4 * NQ].rearrange("p (j q) -> p j q", q=NQ),
                             ACT.Copy).then_inc(turned_sb, 1)


def first_state(nc, m):
    with phase(nc, "turned", "turned_sb", "out_ps", "biased", "ready", "stored") as (
            block, turned, turned_sb, out_ps, biased, ready, stored):
        @block.tensor
        def _(pe):
            turn(nc, m, pe, m.x, 0, turned, turned_sb)
            pe.wait_ge(turned_sb, NC)
            for c in range(NC):
                for j in range(4):
                    mm = nc.tensor.matmul(m.agg[c][:, j * P:(j + 1) * P], m.turned_m[:, 4 * c + j, :], m.lin0,
                                          start=True, stop=True)
            mm.then_inc(out_ps, 1)

        @block.scalar
        def _(act):
            copy_turned(nc, m, act, m.turned_m, 0, turned, turned_sb)
            act.wait_ge(biased, NC)
            nc.scalar.activation(m.h, m.h, ACT.Relu).then_inc(ready, 1)

        @block.vector
        def _(dve):
            dve.wait_ge(out_ps, 1)
            for c in range(NC):
                nc.vector.tensor_tensor(feats(m.h[:, c * WN * D:(c + 1) * WN * D]), feats(m.agg[c]),
                                        by_feature(m.lin0_b, WN), ALU.add).then_inc(biased, 1)

        @block.sync
        def _(sp):
            store_nodes(sp, m, m.h, ready, stored)


def gru(nc, m):
    gates = m.gates.rearrange("q (m g) -> q m g", g=GATE)
    part = lambda j: gates[:, :, j * D:(j + 1) * D]
    with phase(nc, "biased", "relu", "turned", "turned_sb", "gate_ps", "gate_sb", "sig", "pre_n", "tanh",
               "ready", "stored", "own") as (
            block, biased, relu, turned, turned_sb, gate_ps, gate_sb, sig, pre_n, tanh, ready, stored, own):
        @block.vector
        def _(dve):
            V = nc.vector
            do = Chain(dve, own)
            for c in range(NC):
                V.tensor_tensor(feats(m.y[:, c * WN * D:(c + 1) * WN * D]), feats(m.agg[c]),
                                by_feature(m.conv_b, WN), ALU.add).then_inc(biased, 1)
            for g in range(16):
                dve.wait_ge(gate_ps, g + 1)
                V.tensor_tensor(gates[:, 4 * g:4 * g + 4, :], m.ps_p2[g % 2].rearrange("q (m g) -> q m g", g=GATE),
                                m.gate_b.unsqueeze(1).broadcast_to([NQ, 4, GATE]), ALU.add).then_inc(gate_sb, 1)
            dve.wait_ge(sig, 1)
            do(V.tensor_tensor(part(0), part(0), part(3), ALU.mult))
            do(V.tensor_tensor(part(2), part(2), part(0), ALU.add))
            dve.sem_inc(pre_n, 1)
            dve.wait_ge(tanh, 1)
            do(V.tensor_tensor(feats(m.y), feats(m.h), part(2), ALU.subtract))
            do(V.tensor_tensor(feats(m.y), feats(m.y), part(1), ALU.mult))
            do(V.tensor_tensor(feats(m.h), feats(m.y), part(2), ALU.add))
            dve.sem_inc(ready, 1)

        @block.scalar
        def _(act):
            copy_turned(nc, m, act, m.turned_h, 0, turned, turned_sb)
            for c in range(NC):
                act.wait_ge(biased, c + 1)
                piece = m.y[:, c * WN * D:(c + 1) * WN * D]
                nc.scalar.activation(piece, piece, ACT.Relu).then_inc(relu, 1)
            copy_turned(nc, m, act, m.turned_m, 1, turned, turned_sb)
            act.wait_ge(gate_sb, 16)
            nc.scalar.activation(gates[:, :, 0:2 * D], gates[:, :, 0:2 * D], ACT.Sigmoid).then_inc(sig, 1)
            act.wait_ge(pre_n, 1)
            nc.scalar.activation(part(2), part(2), ACT.Tanh).then_inc(tanh, 1)

        @block.tensor
        def _(pe):
            turn(nc, m, pe, m.h, 0, turned, turned_sb)
            pe.wait_ge(relu, NC)
            turn(nc, m, pe, m.y, 1, turned, turned_sb)
            pe.wait_ge(turned_sb, 2 * NC)
            for g in range(16):
                if g >= 2:
                    pe.wait_ge(gate_sb, g - 1)
                nc.tensor.matmul(m.ps_p2[g % 2], m.turned_m[:, g, :], m.gru_i, start=True, stop=False)
                nc.tensor.matmul(m.ps_p2[g % 2], m.turned_h[:, g, :], m.gru_h, start=False,
                                 stop=True).then_inc(gate_ps, 1)

        @block.sync
        def _(sp):
            store_nodes(sp, m, m.h, ready, stored)


def convolve(nc, m):
    first_state(nc, m)
    with nc.Fori(0, STEPS1):
        edge_pass(nc, m, None, m.en2_b, edge_matrices=True)
        add_tiles(nc, m)
        gru(nc, m)
    norm_phase(nc, m)


def scale_and_store(nc, m, by):
    with phase(nc, "ready", "stored", "own") as (block, ready, stored, own):
        @block.vector
        def _(dve):
            Chain(dve, own)(nc.vector.tensor_tensor(feats(m.y), feats(m.x), by_node(by), ALU.mult))
            dve.sem_inc(ready, 1)

        @block.sync
        def _(sp):
            store_nodes(sp, m, m.y, ready, stored)


def graph_conv(nc, m):
    scale_and_store(nc, m, m.inv_out)
    edge_pass(nc, m, None, m.w2)
    add_tiles(nc, m)
    with phase(nc, "own") as (block, own):
        @block.vector
        def _(dve):
            V = nc.vector
            do = Chain(dve, own)
            for c in range(NC):
                do(V.tensor_tensor(feats(m.h[:, c * WN * D:(c + 1) * WN * D]), feats(m.agg[c]),
                                   by_node(m.inv_in[:, c * WN:(c + 1) * WN], WN), ALU.mult))
            do(V.tensor_tensor(feats(m.h), feats(m.h), by_feature(m.b2), ALU.add))
            do(V.tensor_scalar_max(m.h, m.h, 0.0))
    norm_phase(nc, m)


def self_loop_conv(nc, m):
    scale_and_store(nc, m, m.inv_self)
    edge_pass(nc, m, 2, m.ident[0:D, 0:D])
    add_tiles(nc, m)
    with phase(nc, "own") as (block, own):
        @block.vector
        def _(dve):
            V = nc.vector
            do = Chain(dve, own)
            for c in range(NC):
                part = slice(c * WN * D, (c + 1) * WN * D)
                do(V.tensor_tensor(m.h[:, part], m.agg[c], m.y[:, part], ALU.add))
            do(V.tensor_tensor(feats(m.h), feats(m.h), by_node(m.inv_self), ALU.mult))
    norm_phase(nc, m)


def store_result(nc, m, out):
    with phase(nc, "stored") as (block, stored):
        @block.sync
        def _(sp):
            sp.dma_start(out[0:FULL * NM, :].rearrange("(q m) f -> q (m f)", m=NM),
                         m.x[0:FULL, :]).then_inc(stored, 16)
            sp.dma_start(out[FULL * NM:NODES, :].rearrange("(q m) f -> q (m f)", q=1),
                         m.x[FULL:FULL + 1, 0:REST * D]).then_inc(stored, 16)
            sp.wait_ge(stored, 32)


def build(nc, x, src, dst, attr, weight, w, out):
    m = Mem()
    with ExitStack() as whole:
        def make(stack):
            def sb(name, shape, dt=F32, halves=0):
                if halves:
                    return [stack.enter_context(nc.sbuf_tensor(f"sb_{name}{i}", shape, dt))[:] for i in range(halves)]
                return stack.enter_context(nc.sbuf_tensor(f"sb_{name}", shape, dt))[:]
            return sb

        sb = make(whole)
        dram = lambda name, shape, dt=F32: nc.dram_tensor(name, shape, dt, kind="Internal").ap()
        m.slots = dram("slots", [P * TP, ROW])
        m.eh_dram = dram("eh", [P, TP * K])
        m.node_dram = dram("node_rows", [NQ * NM, D])
        m.part_dram = dram("parts", [TP * WN, D])
        m.deg_dram = dram("degree_parts", [3, TP * WN])
        m.row_dram = dram("window_counts", [NW])

        psum = lambda name, n: whole.enter_context(nc.psum_tensor(name, [P, n, 512], F32))[:]
        banks4, banks_s, banks_p = psum("banks4", 4), psum("banks_s", 2), psum("banks_p", 2)
        m.ps_g = banks4
        m.agg = [banks4[0:NQ, c, :] for c in range(NC)]
        m.ps_s = banks_s[0:D, 0, 0:TC * WN]
        m.ps_out = banks_s[:, 1, 0:D]
        m.ps_s2 = [banks_s[:, h, :] for h in range(2)]
        m.ps_pj = [banks_p[:, h, 0:TC * WN] for h in range(2)]
        m.ps_p2 = [banks_p[0:NQ, h, :] for h in range(2)]
        m.ps_count = banks_s[0:HI, 0, 0:LO]
        m.ps_src = banks_s[0:NQ, 1, 0:NM]
        m.ps_rank = [banks4[0:EQ, b, 0:NW] for b in range(2)]
        m.ps_turn = [banks_s[:, g, 0:P] for g in range(2)]
        m.ps_deg = banks4[0:3, 0, 0:TC * WN]
        m.ps_eh = [banks_p[:, g, :] for g in range(2)]
        m.ps_degree = banks4[0:NQ, 1, 0:NC * 3 * WN]

        m.owner = sb("owner", [OQ, OC, NW])
        m.ident = sb("ident", [P, P])
        m.node1, m.fold = sb("node1", [P, WN]), sb("fold", [P, D])
        m.deg_out = sb("deg_out", [NQ, NM])
        m.deg_w, m.positive, m.inv_w, m.inv_self, m.inv_in, m.inv_out, m.stat = (
            sb(n, [NQ, NM]) for n in ("deg_w", "positive", "inv_w", "inv_self", "inv_in", "inv_out", "stat"))

        with ExitStack() as setup:
            sb = make(setup)
            m.src, m.dst = (
                sb(n, [EQ, ET], I32) for n in ("src", "dst"))
            m.tmp_i = sb("tmp_i", [EQ, ET], I32)
            m.wcol, m.win, m.whi, m.wlo, m.shi, m.slo = (
                sb(n, [EQ, ET]) for n in ("wcol", "win", "whi", "wlo", "shi", "slo"))
            m.meta = sb("meta", [EQ, ET * META])
            m.zeros = sb("zeros", [P, OQ * ROW])
            m.iota_i = sb("iota_i", [P, NW], I32)
            m.pcol_i = sb("pcol_i", [P, 1], I32)
            m.iota = sb("iota", [P, NW])
            m.iota_h = sb("iota_h", [P, NW], F16)
            m.pcol = sb("pcol", [P, 1])
            m.tnum = sb("tnum", [P, 1])
            m.earlier = sb("earlier", [P, P], BF16)
            m.others = sb("others", [P, P], BF16)
            m.ones_b = sb("ones_b", [P, P], BF16)
            m.ones_f = sb("ones_f", [1, P])
            m.zero_b = sb("zero_b", [1, P], BF16)
            m.hot_hi = sb("hot_hi", [EQ, HT, HI], BF16, halves=2)
            m.hot_lo = sb("hot_lo", [EQ, HT, LO], BF16, halves=2)
            m.count = sb("count", [HI, LO])
            m.cnt, m.tiles, m.scan0, m.scan1, m.first, m.first_slot = (
                sb(n, [P, NW]) for n in ("cnt", "tiles", "scan0", "scan1", "first", "first_slot"))
            m.cnt_i = sb("cnt_i", [P, NW], I32)
            m.rows = sb("rows", [EQ, ST, ROW], halves=2)
            m.win_now = sb("win_now", [EQ, ST], halves=2)
            m.hot_shi = sb("hot_shi", [EQ, ST, NQ], BF16, halves=2)
            m.hot_slo = sb("hot_slo", [EQ, ST, NM], BF16, halves=2)
            m.ring = sb("ring", [EQ, NW], BF16, halves=4)
            m.junk = sb("junk", [EQ, NW], BF16, halves=2)
            m.slot_f = sb("slot_f", [EQ, ST], halves=2)
            m.slot_u = sb("slot_u", [EQ, ST], U32, halves=2)
            m.slot_i, m.slot_t, m.slot_p = (sb(n, [EQ, ST], I32) for n in ("slot_i", "slot_t", "slot_p"))
            m.slot_tf, m.slot_pf = (sb(n, [EQ, ST]) for n in ("slot_tf", "slot_pf"))
            prepare_edges(nc, m, src, dst, weight)
            count_windows(nc, m)
            place_windows(nc, m)
            scatter_rows(nc, m, attr)

        sb = make(whole)
        m.src_t, m.meta_t = sb("src_t", [P, TP], U32), sb("meta_t", [P, TP * 3])
        m.mask = sb("mask", [P, TC, WN], halves=L)
        m.eh = sb("eh_sb", [P, TC * K], halves=L)
        m.en1, m.en1_b = sb("en1", [P, 4 * K]), sb("en1_b", [P, 4 * K])
        m.x, m.h, m.y = (sb(n, [NQ, NM * D]) for n in ("x_sb", "h_sb", "y_sb"))
        m.en2, m.en2_b, m.w2 = sb("en2", [K, D, D]), sb("en2_b", [D, D]), sb("w2", [D, D])
        m.b2, m.conv_b, m.lin0_b = (sb(n, [NQ, D]) for n in ("b2", "conv_b", "lin0_b"))
        m.lin0 = sb("lin0", [P, P])
        m.gru_i, m.gru_h = sb("gru_i", [P, 4 * GATE]), sb("gru_h", [P, 4 * GATE])
        m.bias_i, m.bias_h, m.gate_b = (sb(n, [NQ, k]) for n, k in (("bias_i", 96), ("bias_h", 96), ("gate_b", GATE)))
        load_everything(nc, m, x, w)

        with ExitStack() as encode:
            sb = make(encode)
            m.rowin = sb("rowin", [P, TC * ROW], halves=L)
            m.attr = sb("attr", [P, TC * D], halves=2)
            m.attr_t = sb("attr_t", [P, P], halves=4)
            m.eh_pre = sb("eh_pre", [P, 4 * K], halves=2)
            m.deg_s = sb("deg_s", [3, TC * WN], halves=L)
            m.deg_t = sb("deg_t", [OQ, OC, 3 * WN])
            encode_edges(nc, m)
            node_degrees(nc, m)

        sb = make(whole)
        m.idx = sb("idx", [P, TC], U32, halves=L)
        m.xs = sb("xs", [P, TC * D], halves=L)
        spread, g = sb("spread", [P, 2, TC, D, WN]), sb("g", [P, 2, D, TC, WN])
        m.spread, m.g = [spread[:, h] for h in range(2)], [g[:, h] for h in range(2)]
        m.parts = spread[0:OQ].rearrange("p h t i n -> p (h t i n)").rearrange("p (ch x) -> p ch x", ch=OC)
        m.gates = g[0:NQ].rearrange("p h i t n -> p (h i t n)")
        m.s = sb("s", [D, TC * WN], halves=2)
        m.part = sb("part", [P, D], halves=L)
        m.pj = sb("pj", [P, P], halves=2)
        m.turned_m, m.turned_h = sb("turned_m", [P, 16, NQ]), sb("turned_h", [P, 16, NQ])
        propagate(nc, m)
        convolve(nc, m)
        graph_conv(nc, m)
        self_loop_conv(nc, m)
        store_result(nc, m, out)


def kernel(x, src, dst, edge_attr_32, edge_weight, L1_gnn_lin0_w, L1_gnn_lin0_b, L1_gnn_en1_w, L1_gnn_en1_b,
           L1_gnn_en2_w, L1_gnn_en2_b, L1_gnn_conv_bias, L1_gnn_gru_wih, L1_gnn_gru_whh, L1_gnn_gru_bih,
           L1_gnn_gru_bhh, L2_gnn_weight, L2_gnn_bias):
    import numpy as np
    import concourse.bacc as bacc
    from concourse.bass_utils import run_bass_kernel_spmd

    nc = bacc.Bacc("TRN2", target_bir_lowering=False, num_devices=1)
    arrays = {}

    def put(name, a):
        arrays[name] = np.ascontiguousarray(a)
        return nc.dram_tensor(name, arrays[name].shape, mybir.dt.from_np(arrays[name].dtype), kind="ExternalInput").ap()

    t = np.transpose
    w = {
        "lin0": put("lin0_t", t(np.asarray(L1_gnn_lin0_w))), "lin0_b": put("lin0_bias", L1_gnn_lin0_b),
        "en1": put("en1_t", t(np.asarray(L1_gnn_en1_w))), "en1_b": put("en1_bias", L1_gnn_en1_b),
        "en2": put("en2_t", t(np.asarray(L1_gnn_en2_w))), "en2_b": put("en2_bias", L1_gnn_en2_b),
        "conv_b": put("conv_bias", L1_gnn_conv_bias),
        "wih": put("wih_t", t(np.asarray(L1_gnn_gru_wih))), "whh": put("whh_t", t(np.asarray(L1_gnn_gru_whh))),
        "bih": put("gru_bih", L1_gnn_gru_bih), "bhh": put("gru_bhh", L1_gnn_gru_bhh),
        "w2": put("conv2_w", L2_gnn_weight), "b2": put("conv2_bias", L2_gnn_bias),
    }
    args = [put("x", x), put("src", src), put("dst", dst), put("edge_attr", edge_attr_32), put("edge_weight", edge_weight)]
    out = nc.dram_tensor("out", (NODES, D), F32, kind="ExternalOutput").ap()
    build(nc, *args, w, out)
    return run_bass_kernel_spmd(nc, [arrays], core_ids=[0]).results[0]["out"]
```
